# Optimizing a Trainium2 kernel written in Bass

```python
import numpy as np
import jax
import jax.numpy as jnp

def _softmax(x, axis=-1):
    return jax.nn.softmax(x, axis=axis)

def _gelu(x):
    return jax.nn.gelu(x, approximate=True)

def _silu(x):
    return jax.nn.silu(x)

def _sigmoid(x):
    return jax.nn.sigmoid(x)

def _layernorm(x, axis=-1, eps=1e-05):
    m = jnp.mean(x, axis=axis, keepdims=True)
    v = jnp.var(x, axis=axis, keepdims=True)
    return (x - m) / jnp.sqrt(v + eps)

def _scatter_add(tgt, idx, src, axis=0):
    return tgt.at[idx].add(src)

def _segment_sum(src, seg, n):
    return jax.ops.segment_sum(src, seg, n)
kernel_name = 'mk_seq_postln_d1_jaxref_r8_61ddaf'

def setup_inputs(seed: int=0):
    np.random.seed(seed)
    _w = jnp.asarray

    def _L0_attn_setup():
        import jax, jax.numpy as jnp
        import numpy as np
        key = jax.random.key(seed)
        ks = jax.random.split(key, 5)
        B, S, D = (2, 256, 128)
        scale = 0.02
        return {'x': jax.random.normal(ks[0], (B, S, D), dtype=jnp.float32), 'q_proj_weight': jax.random.normal(ks[1], (D, D), dtype=jnp.float32) * scale, 'k_proj_weight': jax.random.normal(ks[2], (D, D), dtype=jnp.float32) * scale, 'v_proj_weight': jax.random.normal(ks[3], (D, D), dtype=jnp.float32) * scale, 'o_proj_weight': jax.random.normal(ks[4], (D, D), dtype=jnp.float32) * scale}
    _L0_attn_in = _L0_attn_setup()

    def _L0_ffn_setup():
        import jax, jax.numpy as jnp
        import numpy as np
        H = 128
        I = 64
        E = 64
        G = 8
        TOPK_GROUP = 4
        K = 8
        I_SH = 128
        SCALE = 2.5

        def _route(x, router_w, e_bias):
            T = x.shape[0]
            scores = jax.nn.sigmoid(x.astype(jnp.float32) @ router_w.T.astype(jnp.float32))
            sfc = jax.lax.stop_gradient(scores) + e_bias[None, :]
            group_scores = jax.lax.top_k(sfc.reshape(T, G, E // G), 2)[0].sum(-1)
            _, gidx = jax.lax.top_k(group_scores, TOPK_GROUP)
            gmask = jax.nn.one_hot(gidx, G, dtype=sfc.dtype).sum(1)
            smask = jnp.repeat(gmask, E // G, axis=1)
            masked = jnp.where(smask > 0, sfc, 0.0)
            _, topk_idx = jax.lax.top_k(masked, K)
            w = jnp.take_along_axis(scores, topk_idx, axis=1)
            w = w / (w.sum(-1, keepdims=True) + 1e-20)
            return (topk_idx, w * SCALE)
        key = jax.random.key(seed)
        ks = jax.random.split(key, 9)
        s = 0.02
        return {'hidden_states': jax.random.normal(ks[0], (2, 128, H), jnp.float32), 'router_w': jax.random.normal(ks[1], (E, H), jnp.float32) * s, 'e_bias': jnp.zeros((E,), jnp.float32), 'Wg': jax.random.normal(ks[2], (E, H, I), jnp.float32) * s, 'Wu': jax.random.normal(ks[3], (E, H, I), jnp.float32) * s, 'Wd': jax.random.normal(ks[4], (E, I, H), jnp.float32) * s, 'SWg': jax.random.normal(ks[5], (H, I_SH), jnp.float32) * s, 'SWu': jax.random.normal(ks[6], (H, I_SH), jnp.float32) * s, 'SWd': jax.random.normal(ks[7], (I_SH, H), jnp.float32) * s}
    _L0_ffn_in = _L0_ffn_setup()
    _d = {'L0_attn_x': _L0_attn_in['x'], 'L0_attn_q_proj_weight': _L0_attn_in['q_proj_weight'], 'L0_attn_k_proj_weight': _L0_attn_in['k_proj_weight'], 'L0_attn_v_proj_weight': _L0_attn_in['v_proj_weight'], 'L0_attn_o_proj_weight': _L0_attn_in['o_proj_weight'], 'L0_ffn_router_w': _L0_ffn_in['router_w'], 'L0_ffn_e_bias': _L0_ffn_in['e_bias'], 'L0_ffn_Wg': _L0_ffn_in['Wg'], 'L0_ffn_Wu': _L0_ffn_in['Wu'], 'L0_ffn_Wd': _L0_ffn_in['Wd'], 'L0_ffn_SWg': _L0_ffn_in['SWg'], 'L0_ffn_SWu': _L0_ffn_in['SWu'], 'L0_ffn_SWd': _L0_ffn_in['SWd']}
    _x0 = _d['L0_attn_x']
    _d['L0_attn_x'] = jax.random.normal(jax.random.fold_in(jax.random.key(seed), 1), (8, 512, 128), dtype=_x0.dtype)
    del _x0
    return _d

def reference(L0_attn_x, L0_attn_q_proj_weight, L0_attn_k_proj_weight, L0_attn_v_proj_weight, L0_attn_o_proj_weight, L0_ffn_router_w, L0_ffn_e_bias, L0_ffn_Wg, L0_ffn_Wu, L0_ffn_Wd, L0_ffn_SWg, L0_ffn_SWu, L0_ffn_SWd):

    def _L0_attn_ref(x, q_proj_weight, k_proj_weight, v_proj_weight, o_proj_weight):
        import jax, jax.numpy as jnp
        import numpy as np
        num_heads = 16
        B, S, d_in = x.shape
        d_k = q_proj_weight.shape[0]
        head_size = d_k // num_heads

        def split_heads(t):
            return t.reshape(B, S, num_heads, head_size).transpose(0, 2, 1, 3)
        q = split_heads(jnp.einsum('bsd,kd->bsk', x, q_proj_weight))
        k = split_heads(jnp.einsum('bsd,kd->bsk', x, k_proj_weight))
        v = split_heads(jnp.einsum('bsd,kd->bsk', x, v_proj_weight))
        scale = jnp.float32(head_size) ** (-0.5)
        scores = jnp.einsum('bhtc,bhkc->bhtk', q, k) * scale
        causal = jnp.tril(jnp.ones((S, S), dtype=bool))
        scores = jnp.where(causal, scores, -jnp.inf)
        attn = jax.nn.softmax(scores, axis=-1)
        out = jnp.einsum('bhtk,bhkc->bhtc', attn, v)
        out = out.transpose(0, 2, 1, 3).reshape(B, S, d_k)
        return jnp.einsum('bsv,dv->bsd', out, o_proj_weight)

    def _L0_ffn_ref(hidden_states, router_w, e_bias, Wg, Wu, Wd, SWg, SWu, SWd):
        import jax, jax.numpy as jnp
        import numpy as np
        H = 128
        I = 64
        E = 64
        G = 8
        TOPK_GROUP = 4
        K = 8
        I_SH = 128
        SCALE = 2.5

        def _route(x, router_w, e_bias):
            T = x.shape[0]
            scores = jax.nn.sigmoid(x.astype(jnp.float32) @ router_w.T.astype(jnp.float32))
            sfc = jax.lax.stop_gradient(scores) + e_bias[None, :]
            group_scores = jax.lax.top_k(sfc.reshape(T, G, E // G), 2)[0].sum(-1)
            _, gidx = jax.lax.top_k(group_scores, TOPK_GROUP)
            gmask = jax.nn.one_hot(gidx, G, dtype=sfc.dtype).sum(1)
            smask = jnp.repeat(gmask, E // G, axis=1)
            masked = jnp.where(smask > 0, sfc, 0.0)
            _, topk_idx = jax.lax.top_k(masked, K)
            w = jnp.take_along_axis(scores, topk_idx, axis=1)
            w = w / (w.sum(-1, keepdims=True) + 1e-20)
            return (topk_idx, w * SCALE)
        orig_shape = hidden_states.shape
        x = hidden_states.reshape(-1, orig_shape[-1])
        T = x.shape[0]
        topk_idx, topk_w = _route(x, router_w, e_bias)
        coef = jnp.zeros((T, E), topk_w.dtype).at[jnp.arange(T)[:, None], topk_idx].add(topk_w)
        g = jnp.einsum('th,ehi->tei', x, Wg)
        u = jnp.einsum('th,ehi->tei', x, Wu)
        h = jax.nn.silu(g) * u * coef[:, :, None]
        moe_out = jnp.einsum('tei,eih->th', h, Wd)
        shared = jax.nn.silu(x @ SWg) * (x @ SWu) @ SWd
        return (moe_out + shared).reshape(orig_shape)
    x = L0_attn_x
    x = _layernorm(x + _L0_attn_ref(x, L0_attn_q_proj_weight, L0_attn_k_proj_weight, L0_attn_v_proj_weight, L0_attn_o_proj_weight), axis=-1)
    x = _layernorm(x + _L0_ffn_ref(x, L0_ffn_router_w, L0_ffn_e_bias, L0_ffn_Wg, L0_ffn_Wu, L0_ffn_Wd, L0_ffn_SWg, L0_ffn_SWu, L0_ffn_SWd), axis=-1)
    return x

_drawn_inputs = setup_inputs


def setup_inputs(seed=0):
    import zlib

    import numpy as np

    out = dict(_drawn_inputs(seed))
    spreads = {'L0_ffn_e_bias': (0.0, 0.8)}
    factors = {'L0_attn_q_proj_weight': 8.0,
     'L0_attn_k_proj_weight': 8.0,
     'L0_attn_v_proj_weight': 8.0,
     'L0_attn_o_proj_weight': 8.0,
     'L0_ffn_router_w': 8.0,
     'L0_ffn_Wg': 8.0,
     'L0_ffn_Wu': 8.0,
     'L0_ffn_Wd': 8.0,
     'L0_ffn_SWg': 8.0,
     'L0_ffn_SWu': 8.0,
     'L0_ffn_SWd': 8.0}
    for name, (base, spread) in spreads.items():
        noise = np.random.default_rng([zlib.crc32(name.encode()), seed]).standard_normal(out[name].shape)
        drawn = base * np.exp(spread * noise) if base else spread * noise
        out[name] = jnp.asarray(drawn.astype(out[name].dtype))
    for name, factor in factors.items():
        out[name] = (out[name] * factor).astype(out[name].dtype)
    return out
```

```python
import math
from contextlib import ExitStack

import concourse.bass as bass
from concourse import mybir

F32 = mybir.dt.float32
F32R = mybir.dt.float32r
BF16 = mybir.dt.bfloat16
ALU = mybir.AluOpType
ACT = mybir.ActivationFunctionType
AX_X = mybir.AxisListType.X

P = 128
B, S, D = 8, 512, 128
NH, C = 16, 8
NT = S // P
E, I = 64, 64
PAIRS = E * I // P
SHARED = 0
UNITS = PAIRS + 1
NG = 8
GE = E // NG
TOPG, TOPK = 4, 8
ROUTE_SCALE = 2.5
EPS = 1e-5
HG = 4
GROUPS = NH // HG
PARTS = 3
QK_ROWS = PARTS * PARTS * C
STACK = 96
VW = C + 1
VPAD = NH * VW + 32 - VW
BIG = 3.0e38
FOUND = 1.0e38
EH = 32
HEAD_COLS = 1280
KB_AT = (0, 512, 1024, 896)
ST_PARTS = ((0,), (1, 3), (2,))
MX_PARTS = ((0, 1), (2,), (3,))

MAX_AT, ST_AT = -52, -42


def attention_places():
    out = [(-62, "ld", 0), (-58, "q", 0), (-57, "k", 0), (-56, "v", 0), (-12, "ldtok", 0)]
    for g, at in enumerate((-55, -54, -52, -44)):
        out.append((at + 0.05, "rs", g))
    for h in range(NH):
        for part, off in enumerate((0.1, 0.65, 1.1)):
            out.append((MAX_AT + 2 * h + off, "mx", 3 * h + part))
        for part, off in enumerate((0.4, 0.9, 1.4)):
            out.append((ST_AT + 2 * h + off, "st", 3 * h + part))
        out.append((ST_AT + 2 * h + 1.45, "mask", h))
    for g in range(GROUPS):
        out.append((MAX_AT + 8 * g + 7.7, "mn", g))
        out.append((MAX_AT + 8 * g + 8.3, "mT", g))
        out.append((ST_AT + 8 * g + 8.2, "pv", g))
        out.append((ST_AT + 8 * g + 8.95, "ot", g))
    out += [(-7.9, "attT", 0), (-6.9, "oproj", 0), (-5.9, "x1", 0), (-5.2, "x1T", 0),
            (-4.3, "router", 0), (-3.9, "tk", 0), (-3.4, "tk", 1), (-2.9, "tk", 2), (-2.4, "tk", 3),
            (-1.3, "coefT", 0)]
    return out


def moe_places():
    out = []
    for u in range(UNITS):
        out += [(u, "g", u), (u + 0.25, "u", u), (u + 0.3, "a", u), (u + 0.55, "b", u),
                (u + 1.8, "d", u)]
        if u != SHARED:
            out += [(u + 0.5, "c", u), (u + 0.6, "h", u)]
    out += [(UNITS + 0.9, "fin", 0), (UNITS + 1.3, "finT", 0), (UNITS + 2.3, "finx", 0)]
    return out


def order(first_step, last_step, batch_ok):
    out = []
    for n in range(first_step - 2, last_step + 3):
        for at, kind, i in attention_places() + moe_places():
            t = n * UNITS + at
            step = math.floor(t / UNITS)
            moe = at >= 0
            if not batch_ok(n):
                continue
            if moe and first_step <= n <= last_step:
                out.append((t, kind, n, i))
            elif not moe and first_step <= step <= last_step:
                out.append((t, kind, n, i))
    out.sort(key=lambda x: x[0])
    return [(kind, n, i) for _, kind, n, i in out]


BANK_SM = ("q", "k", "v", "mx", "mT")
BANK_O = ("pv", "ot", "attT", "oproj", "x1T", "router", "coefT", "finT")
LN = ("oproj", "finT")


class Segment:

    def __init__(self, tasks):
        self.tasks = tasks
        self.numbers = {}
        for kinds in (BANK_SM, BANK_O, LN, ("q", "k")) + tuple((k,) for k in {t[0] for t in tasks}):
            here = [t for t in tasks if t[0] in kinds]
            self.numbers[kinds] = {t: n + 1 for n, t in enumerate(here)}

    def nth(self, kinds, task):
        return self.numbers.get(kinds, {}).get(task, 0)

    def total(self, kinds):
        return len(self.numbers.get(kinds, {}))


def build(nc, x, xT, wqT, wkT, wvT, woT, rwT, bias, Wg, Wu, Wd, SWg, SWu, SWd, ident, causal, select, out):
    x_tok = x.rearrange("(b t p) d -> b p t d", t=NT, p=P)
    out_tok = out.rearrange("(b t p) d -> b p t d", t=NT, p=P)
    q_parts_dram = nc.dram_tensor("q_parts_dram", [NH, PARTS, C, S], BF16).ap()
    k_parts_dram = nc.dram_tensor("k_parts_dram", [NH, PARTS, C, S], BF16).ap()

    PRO = Segment(order(-2, -1, lambda n: n >= 0))
    BODY = Segment(order(0, 1, lambda n: n >= 0))
    EPI = Segment(order(6, 7, lambda n: n < B))
    BODY_RUNS = (B - 2) // 2

    with ExitStack() as ctx:
        def sb(name, shape, dt=F32):
            return ctx.enter_context(nc.sbuf_tensor(name, shape, dt))

        def bank(name):
            return ctx.enter_context(nc.psum_tensor(name, [P, 512], F32))

        sems = []

        def sem(name):
            s = ctx.enter_context(nc.semaphore(name))
            sems.append(s)
            return s

        wg_hi, wg_lo = sb("wg_hi", [P, E * I], F32R), sb("wg_lo", [P, E * I], F32R)
        wu_hi, wu_lo = sb("wu_hi", [P, E * I], F32R), sb("wu_lo", [P, E * I], F32R)
        wd_sb = sb("wd_sb", [P, PAIRS * D])
        sg_hi, sg_lo = sb("sg_hi", [P, P], F32R), sb("sg_lo", [P, P], F32R)
        su_hi, su_lo = sb("su_hi", [P, P], F32R), sb("su_lo", [P, P], F32R)
        sd_sb = sb("sd_sb", [P, D])
        wq_sb, wk_sb, wv_sb, wo_sb = (sb(f"w{n}_sb", [P, D]) for n in "qkvo")
        rw_sb = sb("rw_sb", [P, E])
        bias_sb = sb("bias_sb", [P, E])
        id_sb = sb("id_sb", [P, P])
        id_bf = sb("id_bf", [P, P], BF16)
        causal_sb = sb("causal_sb", [P, S], BF16)
        select_sb = sb("select_sb", [STACK, PAIRS // 2, P], BF16)
        half_power = sb("half_power", [P, NT])
        xT_sb = sb("xT_sb", [P, S])
        xtok_sb = sb("xtok_sb", [P, NT, D])
        qk_parts = sb("qk_parts", [P, PARTS, S], BF16)
        rest = sb("rest", [P, S])
        q_stack = sb("q_stack", [STACK, NH, S], BF16)
        k_stack = sb("k_stack", [STACK, NH, S], BF16)
        v_sb = sb("v_sb", [P, 2, NT, VPAD])
        max_out = sb("max_out", [P, S], BF16)
        row_max = sb("row_max", [P, HG, NT])
        max_rest = sb("max_rest", [P, HG * NT])
        max_parts = sb("max_parts", [P, PARTS, HG * NT], BF16)
        max_rows = sb("max_rows", [PARTS * HG * NT, P], BF16)
        probs = sb("probs", [P, HG, HEAD_COLS])
        ev = sb("ev", [P, S])
        rden = sb("rden", [P, NT, HG])
        att = sb("att", [P, NT, D])
        y = sb("y", [P, NT, D])
        stats = sb("stats", [P, NT, 6])
        mv = sb("mv", [P, NT, 2])
        var_eps = sb("var_eps", [P, NT])
        rstd = sb("rstd", [P, NT])
        x1 = sb("x1", [P, 2, NT, D])
        x1T = sb("x1T", [P, S])
        th = sb("th", [P, NT, E])
        sfc = sb("sfc", [P, NT * E])
        pair_hi = sb("pair_hi", [P, NT * NG * 4])
        pair_lo = sb("pair_lo", [P, NT * NG * 4])
        quad_a = sb("quad_a", [P, NT * NG * 2])
        quad_b = sb("quad_b", [P, NT * NG * 2])
        gs = sb("gs", [P, NT, NG + TOPG])
        g_top = sb("g_top", [P, NT, 8])
        g_keep = sb("g_keep", [P, NT, 8])
        g_found = sb("g_found", [P, NT, NG + TOPG])
        merge_tmp = sb("merge_tmp", [P, NT * NG * 2])
        g_mask = sb("g_mask", [P, NT, NG])
        e_top = sb("e_top", [P, NT, 8])
        chosen = sb("chosen", [P, NT, E])
        w_sum = sb("w_sum", [P, NT])
        coef_parts = sb("coef_parts", [P, NT, 2, PARTS, EH], BF16)
        coef_T = sb("coef_T", [STACK, 2, 2, S], BF16)
        x1_hi, x1_lo = sb("x1_hi", [P, 2, S], F32R), sb("x1_lo", [P, 2, S], F32R)
        hid = sb("hid", [P, 3, S])
        coef_b = sb("coef_b", [P, 2, S])
        ffn_T = sb("ffn_T", [P, S])
        out_sb = sb("out_sb", [P, NT, D])

        acc, pg, pu, pc = bank("acc"), bank("pg"), bank("pu"), bank("pc")
        sm, st0, st1, ob = bank("sm"), bank("st0"), bank("st1"), bank("ob")
        st_bank = (st0, st1)

        x_in = sem("x_in")
        xtok_in = sem("xtok_in")
        sm_full, sm_free = sem("sm_full"), sem("sm_free")
        ob_full, ob_free = sem("ob_full"), sem("ob_free")
        part1_done = sem("part1_done")
        parts_done = sem("parts_done")
        parts_stored = sem("parts_stored")
        stacked = [sem(f"stacked{g}") for g in range(GROUPS)]
        maxparts_done = sem("maxparts_done")
        maxrows_in = [sem(f"maxrows_in{g}") for g in range(GROUPS)]
        st_full, exp_done = sem("st_full"), sem("exp_done")
        probs_ready = sem("probs_ready")
        var_done, rstd_done, x1_done = sem("var_done"), sem("rstd_done"), sem("x1_done")
        x1hi_done, coefparts_done = sem("x1hi_done"), sem("coefparts_done")
        g_full, u_full, c_full, d_full = sem("g_full"), sem("u_full"), sem("c_full"), sem("d_full")
        tanh_done, a_done, b_done = sem("tanh_done"), sem("a_done"), sem("b_done")
        c_copied, h_done = sem("c_copied"), sem("h_done")
        acc_free = sem("acc_free")
        out_ready, out_stored = sem("out_ready"), sem("out_stored")
        dve_step = sem("dve_step")
        w_in = sem("w_in")
        wd_in = sem("wd_in")
        stage_in = [sem(f"stage_in{j}") for j in range(3)]
        stage_hi, stage_used = sem("stage_hi"), sem("stage_used")
        const_done = sem("const_done")
        seg_done = ctx.enter_context(nc.semaphore("seg_done"))
        seg_go = ctx.enter_context(nc.semaphore("seg_go"))
        seg_ack = ctx.enter_context(nc.semaphore("seg_ack"))

        CH = 512
        chunks = []
        for src, hi, lo in ((SWg, sg_hi, sg_lo), (SWu, su_hi, su_lo)):
            chunks.append((src, hi[:, :], lo[:, :], P, P))
        sel_v = select_sb[:, :, :].rearrange("p a b -> p (a b)")
        for c in range(E * I // CH):
            cs = slice(c * CH, (c + 1) * CH)
            chunks.append((Wg[:, cs], wg_hi[:, cs], wg_lo[:, cs], P, CH))
            chunks.append((Wu[:, cs], wu_hi[:, cs], wu_lo[:, cs], P, CH))
        for c in range(PAIRS // 2 * P // CH):
            cs = slice(c * CH, (c + 1) * CH)
            chunks.append((select[:, cs], sel_v[:, cs], None, STACK, CH))
        pro, k = [], 0
        first = next(i for i, t in enumerate(PRO.tasks) if t[0] == "q")
        every = max(1, (len(PRO.tasks) - first) // (len(chunks) + 6))
        for i, t in enumerate(PRO.tasks):
            pro.append(t)
            if i > first + 4 and (i - first) % every == 0 and k < len(chunks):
                pro.append(("chunk", 0, k))
                k += 1
        pro += [("chunk", 0, j) for j in range(k, len(chunks))]
        PRO_ = Segment(pro)

        small = [(wq_sb, wqT), (wk_sb, wkT), (wv_sb, wvT), (wo_sb, woT), (rw_sb, rwT),
                 (bias_sb, bias.unsqueeze(0).to_broadcast([P, E])), (sd_sb, SWd), (id_sb, ident)]

        block = ctx.enter_context(nc.Block())

        def after(eng, seg, s, kinds, task, per=1):
            n = seg.nth(kinds, task)
            if n:
                eng.wait_ge(s, n * per)

        def bank_free(eng, seg, s, kinds, task, banks=1):
            n = seg.nth(kinds, task) - banks
            if n > 0:
                eng.wait_ge(s, n)

        def group_nth(seg, kind, n, g):
            return sum(t[0] == kind and t[2] == g and t[1] <= n for t in seg.tasks)

        def end_segment(eng):
            eng.drain().then_inc(seg_done, 1)
            eng.wait_ge(seg_go, 1)
            eng.sem_inc(seg_ack, 1)

        def run(eng, tasks_of, last_too=False):
            tasks_of(PRO_, 0)
            end_segment(eng)
            with eng.Fori(0, BODY_RUNS) as i:
                tasks_of(BODY, i * 2)
                end_segment(eng)
            tasks_of(EPI, 0)

        @block.sync
        def _(sp):
            for dst, src in small:
                sp.dma_start(dst[:, :], src).then_inc(w_in, 16)
            sp.dma_start(hid[:, 2, :], causal).then_inc(w_in, 16)

            def load_chunk(j):
                src, _, _, rows, cols = chunks[j]
                if j >= 2:
                    sp.wait_ge(stage_used, j - 1)
                sp.dma_start(hid[0:rows, j % 2, 0:cols], src).then_inc(stage_in[j % 2], 16)

            def tasks(seg, base):
                for kind, n, i in seg.tasks:
                    if kind == "chunk":
                        if i == 0:
                            sp.dma_start(wd_sb[:, :], Wd).then_inc(wd_in, 16)
                            load_chunk(0)
                        if i + 1 < len(chunks):
                            load_chunk(i + 1)
                    if kind == "ld":
                        after(sp, seg, sm_full, BANK_SM, ("v", n - 1, 0))
                        sp.dma_start(xT_sb[:, :], xT[base + n]).then_inc(x_in, 16)
                    if kind == "ldtok":
                        after(sp, seg, ob_free, BANK_O, ("oproj", n - 1, 0))
                        sp.dma_start(xtok_sb[:, :, :], x_tok[base + n]).then_inc(xtok_in, 16)
                    if kind in "qk":
                        after(sp, seg, parts_done, ("q", "k"), (kind, n, i))
                        for g in range(GROUPS):
                            if seg.nth(("rs",), ("rs", n - 1, g)):
                                sp.wait_ge(stacked[g], 16 * 12 * group_nth(seg, "rs", n - 1, g))
                        dram = q_parts_dram if kind == "q" else k_parts_dram
                        for p in range(PARTS):
                            sp.dma_start(dram[:, p, :, :], qk_parts[:, p, :]).then_inc(parts_stored, 16)
                    if kind == "rs":
                        after(sp, seg, parts_stored, ("q", "k"), ("k", n, 0), 16 * PARTS)
                        after(sp, seg, st_full, ("st",), ("st", n - 1, 3 * (HG * i + HG) - 1))
                        hs = slice(HG * i, HG * i + HG)
                        for a in range(PARTS):
                            rows = slice(a * PARTS * C, (a + 1) * PARTS * C)
                            for b in range(PARTS):
                                r0 = (a * PARTS + b) * C
                                sp.dma_start(q_stack[r0:r0 + C, hs, :],
                                             q_parts_dram[hs, a].rearrange("h c t -> c h t"))\
                                    .then_inc(stacked[i], 16)
                            sp.dma_start(k_stack[rows, hs, :],
                                         k_parts_dram[hs].rearrange("h b c t -> (b c) h t"))\
                                .then_inc(stacked[i], 16)
                    if kind == "mT":
                        after(sp, seg, sm_free, BANK_SM, (kind, n, i))
                        for a in range(PARTS):
                            src = max_rows[a * HG * NT:(a + 1) * HG * NT, :]
                            dst = q_stack[QK_ROWS + a:QK_ROWS + a + 1, HG * i:HG * i + HG, :]
                            sp.dma_start(dst.rearrange("p h (t q) -> p (h t) q", q=P), src)\
                                .then_inc(maxrows_in[i], 16)
                    if kind == "finx":
                        after(sp, seg, out_ready, ("finx",), (kind, n, i))
                        sp.dma_start(out_tok[base + n], out_sb[:, :, :]).then_inc(out_stored, 16)

            def finish(seg, last=False):
                if seg is PRO_:
                    sp.wait_ge(w_in, 16 * (len(small) + 1))
                    sp.wait_ge(wd_in, 16)
                for s, kinds, per in ((x_in, ("ld",), 16), (xtok_in, ("ldtok",), 16),
                                      (parts_stored, ("q", "k"), 16 * PARTS), (out_stored, ("finx",), 16)):
                    if seg.total(kinds):
                        sp.wait_ge(s, seg.total(kinds) * per)
                for g in range(GROUPS):
                    for s, kind, per in ((stacked[g], "rs", 16 * 12), (maxrows_in[g], "mT", 16 * PARTS)):
                        many = sum(t[0] == kind and t[2] == g for t in seg.tasks)
                        if many:
                            sp.wait_ge(s, many * per)
                if last:
                    return
                sp.wait_ge(seg_done, 4)
                for s in sems:
                    sp.sem_clear(s)
                sp.sem_clear(seg_done)
                sp.sem_inc(seg_go, 1)
                sp.wait_ge(seg_ack, 4)
                sp.sem_clear(seg_go)
                sp.sem_clear(seg_ack)

            tasks(PRO_, 0)
            finish(PRO_)
            with sp.Fori(0, BODY_RUNS) as i:
                tasks(BODY, i * 2)
                finish(BODY)
            tasks(EPI, 0)
            finish(EPI, last=True)

        @block.tensor
        def _(pe):
            def split_products(psum, hi, lo, par, first=True):
                pe.matmul(psum[:, :], hi, x1_hi[:, par, :], start=True, stop=False)
                pe.matmul(psum[:, :], hi, x1_lo[:, par, :], start=False, stop=False)
                return pe.matmul(psum[:, :], lo, x1_hi[:, par, :], start=False, stop=True)

            def tasks(seg, base):
                for kind, n, i in seg.tasks:
                    task = (kind, n, i)
                    par = n % 2
                    if kind in BANK_SM:
                        bank_free(pe, seg, sm_free, BANK_SM, task)
                    if kind in BANK_O:
                        bank_free(pe, seg, ob_free, BANK_O, task)
                    if kind == "q" and seg is PRO_ and n == 0:
                        pe.wait_ge(w_in, 16 * (len(small) + 1))
                        pe.wait_ge(const_done, 5)
                    if kind in ("q", "k"):
                        after(pe, seg, x_in, ("ld",), ("ld", n, 0), 16)
                        w = wq_sb if kind == "q" else wk_sb
                        pe.matmul(sm[:, :], w[:, :], xT_sb[:, :], start=True, stop=True).then_inc(sm_full, 1)
                    if kind == "v":
                        for t in range(NT):
                            mm = pe.matmul(sm[:, t * P:(t + 1) * P], xT_sb[:, t * P:(t + 1) * P], wv_sb[:, :],
                                           start=True, stop=True)
                        mm.then_inc(sm_full, 1)
                    if kind == "mx":
                        h, part = divmod(i, 3)
                        if i % (3 * HG) == 0 and seg.nth(("rs",), ("rs", n, h // HG)):
                            pe.wait_ge(stacked[h // HG], 16 * 12 * group_nth(seg, "rs", n, h // HG))
                        col = 0
                        for qb in MX_PARTS[part]:
                            wide = (qb + 1) * P
                            mm = pe.matmul(sm[:, col:col + wide], q_stack[0:QK_ROWS, h, qb * P:(qb + 1) * P],
                                           k_stack[0:QK_ROWS, h, 0:wide], start=True, stop=True)
                            col += wide
                        mm.then_inc(sm_full, 1)
                    if kind == "mT":
                        after(pe, seg, maxparts_done, ("mn",), ("mn", n, i))
                        pe.transpose(sm[0:PARTS * HG * NT, 0:P // 2].bitcast(BF16),
                                     max_parts[:, :, :].rearrange("p a b -> p (a b)"), id_bf[:, :])\
                            .then_inc(sm_full, 1)
                    if kind == "st":
                        h, part = divmod(i, 3)
                        if i % (3 * HG) == 0 and seg.nth(("mT",), ("mT", n, h // HG)):
                            pe.wait_ge(maxrows_in[h // HG], 16 * PARTS * group_nth(seg, "mT", n, h // HG))
                        bank_free(pe, seg, exp_done, ("st",), task, banks=2)
                        col = 0
                        for kb in ST_PARTS[part]:
                            wide = S - kb * P
                            mm = pe.matmul(st_bank[i % 2][:, col:col + wide], k_stack[:, h, kb * P:(kb + 1) * P],
                                           q_stack[:, h, kb * P:S], start=True, stop=True)
                            col += wide
                        mm.then_inc(st_full, 1)
                    if kind == "pv":
                        after(pe, seg, probs_ready, ("mask",), ("mask", n, HG * i + HG - 1))
                        after(pe, seg, sm_free, BANK_SM, ("v", n, 0))
                        for kb in range(NT):
                            wide = S - kb * P
                            for j in range(HG):
                                c0 = (HG * i + j) * VW
                                mm = pe.matmul(ob[32 * j:32 * j + 32, kb * P:S], v_sb[:, par, kb, c0:c0 + 32],
                                               probs[:, j, KB_AT[kb]:KB_AT[kb] + wide],
                                               start=(kb == 0), stop=(kb == NT - 1))
                        mm.then_inc(ob_full, 1)
                    if kind == "ot" or kind == "attT" or kind == "x1T" or kind == "finT":
                        if kind == "x1T":
                            after(pe, seg, x1_done, ("x1",), ("x1", n, 0))
                        if kind == "finT":
                            after(pe, seg, acc_free, ("fin",), ("fin", n, 0))
                        for t in range(NT):
                            src = {"ot": ev[:, t * P:(t + 1) * P], "attT": att[:, t, :],
                                   "x1T": x1[:, par, t, :], "finT": ffn_T[:, t * P:(t + 1) * P]}[kind]
                            mm = pe.transpose(ob[:, t * P:(t + 1) * P], src, id_sb[:, :])
                        mm.then_inc(ob_full, 1)
                    if kind == "oproj" or kind == "router":
                        lhs, rhs, wide = (ev, wo_sb, D) if kind == "oproj" else (x1T, rw_sb, E)
                        for t in range(NT):
                            mm = pe.matmul(ob[:, t * wide:(t + 1) * wide], lhs[:, t * P:(t + 1) * P], rhs[:, :],
                                           start=True, stop=True)
                        mm.then_inc(ob_full, 1)
                    if kind == "coefT":
                        after(pe, seg, coefparts_done, ("coefT",), task)
                        for f in range(2):
                            for t in range(NT):
                                col = (f * S + t * P) // 2
                                mm = pe.transpose(ob[0:STACK, col:col + P // 2].bitcast(BF16),
                                                  coef_parts[:, t, f, :, :].rearrange("p a e -> p (a e)"),
                                                  id_bf[:, :])
                        mm.then_inc(ob_full, 1)
                    if kind == "g":
                        bank_free(pe, seg, a_done, ("g",), task)
                        after(pe, seg, ob_free, BANK_O, ("x1T", n, 0))
                        w = slice((i - 1) * P, i * P)
                        hi, lo = (sg_hi[:, :], sg_lo[:, :]) if i == SHARED else (wg_hi[:, w], wg_lo[:, w])
                        split_products(pg, hi, lo, par).then_inc(g_full, 1)
                    if kind == "u":
                        bank_free(pe, seg, b_done, ("u",), task)
                        w = slice((i - 1) * P, i * P)
                        hi, lo = (su_hi[:, :], su_lo[:, :]) if i == SHARED else (wu_hi[:, w], wu_lo[:, w])
                        split_products(pu, hi, lo, par).then_inc(u_full, 1)
                    if kind == "c":
                        bank_free(pe, seg, c_copied, ("c",), task)
                        after(pe, seg, ob_free, BANK_O, ("coefT", n, 0))
                        f, p = divmod(i - 1, PAIRS // 2)
                        pe.matmul(pc[:, :], select_sb[:, p, :], coef_T[:, par, f, :], start=True, stop=True)\
                            .then_inc(c_full, 1)
                    if kind == "d":
                        if i == SHARED:
                            after(pe, seg, b_done, ("b",), ("b", n, i))
                            after(pe, seg, acc_free, ("fin",), ("fin", n - 1, 0))
                        else:
                            after(pe, seg, h_done, ("h",), ("h", n, i))
                        w = sd_sb[:, :] if i == SHARED else wd_sb[:, (i - 1) * D:i * D]
                        pe.matmul(acc[:, :], w, hid[:, i % 3, :], start=(i == 0), stop=(i == UNITS - 1))\
                            .then_inc(d_full, 1)

            run(pe, tasks)

        @block.scalar
        def _(act):
            def tasks(seg, base):
                for kind, n, i in seg.tasks:
                    task = (kind, n, i)
                    par = n % 2
                    if kind == "chunk" and chunks[i][2] is not None:
                        _, hi, lo, rows, cols = chunks[i]
                        act.wait_ge(stage_in[i % 2], 16 * (i // 2 + 1))
                        act.activation(hi, hid[0:rows, i % 2, 0:cols], ACT.Copy).then_inc(stage_hi, 1)
                    if kind in ("q", "k"):
                        after(act, seg, sm_full, BANK_SM, task)
                        many = seg.nth(("q", "k"), task) - 1
                        if many:
                            act.wait_ge(parts_stored, 16 * PARTS * many)
                        act.activation(qk_parts[:, 0, :], sm[:, :], ACT.Copy).then_inc(part1_done, 1)
                    if kind == "st":
                        h, part = divmod(i, 3)
                        after(act, seg, st_full, ("st",), task)
                        if part == 0 and h % HG == 0:
                            before = ("pv", n, h // HG - 1) if h else ("pv", n - 1, GROUPS - 1)
                            after(act, seg, ob_full, BANK_O, before)
                        wide = sum(S - kb * P for kb in ST_PARTS[part])
                        at = KB_AT[ST_PARTS[part][0]]
                        act.activation(probs[:, h % HG, at:at + wide], st_bank[i % 2][:, 0:wide], ACT.Exp,
                                       scale=C ** -0.5).then_inc(exp_done, 1)
                    if kind in ("pv", "attT"):
                        after(act, seg, ob_full, BANK_O, task)
                        act.activation(ev[:, :], ob[:, :], ACT.Copy).then_inc(ob_free, 1)
                    if kind == "x1T":
                        after(act, seg, ob_full, BANK_O, task)
                        act.activation(x1T[:, :], ob[:, :], ACT.Copy)
                        after(act, seg, u_full, ("u",), ("u", n - 2, UNITS - 1))
                        act.activation(x1_hi[:, par, :], ob[:, :], ACT.Copy).then_inc(x1hi_done, 1)
                    if kind == "router":
                        after(act, seg, ob_full, BANK_O, task)
                        act.activation(th[:, :, :].rearrange("p t e -> p (t e)"), ob[:, 0:NT * E], ACT.Tanh,
                                       scale=0.5).then_inc(ob_free, 1)
                    if kind == "coefT":
                        after(act, seg, ob_full, BANK_O, task)
                        after(act, seg, c_full, ("c",), ("c", n - 2, UNITS - 1))
                        act.activation(coef_T[:, par, :, :].rearrange("p f t -> p (f t)"),
                                       ob[0:STACK, :].bitcast(BF16), ACT.Copy).then_inc(ob_free, 1)
                    if kind == "g":
                        after(act, seg, g_full, ("g",), task)
                        before = ("d", n, i - 3) if i >= 3 else ("d", n - 1, UNITS + i - 3)
                        after(act, seg, d_full, ("d",), before)
                        act.activation(hid[:, i % 3, :], pg[:, :], ACT.Tanh, scale=0.5).then_inc(tanh_done, 1)
                    if kind == "c":
                        after(act, seg, c_full, ("c",), task)
                        before = ("h", n, i - 2) if i >= 3 else ("h", n - 1, UNITS + i - 3)
                        after(act, seg, h_done, ("h",), before)
                        act.activation(coef_b[:, i % 2, :], pc[:, :], ACT.Copy).then_inc(c_copied, 1)
                    if kind == "fin":
                        after(act, seg, d_full, ("d",), ("d", n, UNITS - 1))
                        after(act, seg, ob_full, BANK_O, ("finT", n - 1, 0))
                        act.activation(ffn_T[:, :], acc[:, :], ACT.Copy).then_inc(acc_free, 1)

            run(act, tasks)

        @block.gpsimd
        def _(pool):
            pool.memset(half_power[:, :], -0.5).then_inc(const_done, 1)

            def tasks(seg, base):
                for kind, n, i in seg.tasks:
                    task = (kind, n, i)
                    if kind == "mask":
                        after(pool, seg, exp_done, ("st",), ("st", n, 3 * i + 2))
                        blocks = probs[:, i % HG, :].rearrange("p (a b) -> p a b", b=P)
                        for diagonal in (blocks[:, 0:5:4, :], blocks[:, 7:9, :]):
                            ins = pool.affine_select(out=diagonal, in_=diagonal, compare_op=ALU.is_ge, fill=0.0,
                                                     base=0, pattern=[[0, 2], [1, P]], channel_multiplier=-1)
                        ins.then_inc(probs_ready, 1)
                    if kind in LN:
                        after(pool, seg, var_done, LN, task)
                        pool.tensor_tensor(rstd[:, :], var_eps[:, :], half_power[:, :], ALU.pow)\
                            .then_inc(rstd_done, 1)
                    if kind == "h":
                        after(pool, seg, b_done, ("b",), ("b", n, i))
                        after(pool, seg, c_copied, ("c",), ("c", n, i))
                        pool.tensor_tensor(hid[:, i % 3, :], hid[:, i % 3, :], coef_b[:, i % 2, :], ALU.mult)\
                            .then_inc(h_done, 1)

            run(pool, tasks)

        @block.vector
        def _(dve):
            steps = [0]

            def done(ins):
                steps[0] += 1
                ins.then_inc(dve_step, 1)
                dve.wait_ge(dve_step, steps[0])

            dve.memset(v_sb[:, :, :, :], 0.0).then_inc(dve_step, 1)
            steps[0] += 1
            dve.wait_ge(dve_step, 1)
            for par in range(2):
                ones = v_sb[:, par, :, 0:NH * VW].rearrange("p t (h e) -> p t h e", e=VW)[:, :, :, C]
                dve.memset(ones, 1.0)
            dve.memset(gs[:, :, NG:NG + TOPG], -BIG)
            done(dve.memset(g_keep[:, :, TOPG:8], -BIG))
            dve.memset(k_stack[64:STACK, :, :], 1.0).then_inc(const_done, 1)
            dve.memset(q_stack[64:STACK, :, :], 0.0).then_inc(const_done, 1)
            dve.wait_ge(w_in, 16 * (len(small) + 1))
            dve.tensor_copy(id_bf[:, :], id_sb[:, :]).then_inc(const_done, 1)
            dve.tensor_copy(causal_sb[:, :], hid[:, 2, :]).then_inc(const_done, 1)
            dve.wait_ge(const_done, 5)

            def norm_stats(seg, task, summed):
                after(dve, seg, ob_full, BANK_O, task)
                dve.tensor_tensor(y[:, :, :].rearrange("p t d -> p (t d)"), ob[:, :],
                                  summed.rearrange("p t d -> p (t d)"), ALU.add).then_inc(ob_free, 1)
                dve.wait_ge(ob_free, seg.nth(BANK_O, task))
                for t in range(NT):
                    last = dve.bn_stats(stats[:, t, :], y[:, t, :])
                done(last)
                for t in range(NT):
                    last = dve.bn_aggr(mv[:, t, :], stats[:, t, :])
                done(last)
                dve.tensor_scalar(var_eps[:, :], mv[:, :, 1], EPS, None, ALU.add).then_inc(var_done, 1)

            def normalise(seg, task, dst, s):
                after(dve, seg, rstd_done, LN, task)
                for t in range(NT):
                    last = dve.tensor_scalar(dst[:, t, :], y[:, t, :], mv[:, t, 0:1], rstd[:, t:t + 1],
                                             ALU.subtract, ALU.mult)
                last.then_inc(s, 1)

            def group_scores():
                done(dve.tensor_scalar(th[:, :, :], th[:, :, :], 0.5, 0.5, ALU.mult, ALU.add))
                done(dve.tensor_tensor(sfc[:, :].rearrange("p (t e) -> p t e", t=NT), th[:, :, :],
                                       bias_sb[:, :].unsqueeze(1).to_broadcast([P, NT, E]), ALU.add))
                a, b = (sfc[:, :].rearrange("p (g e) -> p g e", e=2)[:, :, j] for j in range(2))
                dve.tensor_tensor(pair_hi[:, :], a, b, ALU.max)
                done(dve.tensor_tensor(pair_lo[:, :], a, b, ALU.min))

            def merge(n_in, hi, lo, hi_out, lo_out, both):
                h = [hi[:, 0:n_in].rearrange("p (g e) -> p g e", e=2)[:, :, j] for j in range(2)]
                l = [lo[:, 0:n_in].rearrange("p (g e) -> p g e", e=2)[:, :, j] for j in range(2)]
                m = n_in // 2
                dve.tensor_tensor(both[:, 0:m], l[0], l[1], ALU.max)
                dve.tensor_tensor(hi_out[:, 0:m], h[0], h[1], ALU.max)
                done(dve.tensor_tensor(lo_out[:, 0:m], h[0], h[1], ALU.min))
                done(dve.tensor_tensor(lo_out[:, 0:m], lo_out[:, 0:m], both[:, 0:m], ALU.max))

            def keep_groups():
                merge(NT * NG * 4, pair_hi, pair_lo, quad_a, quad_b, merge_tmp)
                merge(NT * NG * 2, quad_a, quad_b, pair_hi, pair_lo, merge_tmp)
                done(dve.tensor_tensor(gs[:, :, 0:NG], pair_hi[:, 0:NT * NG].rearrange("p (t g) -> p t g", t=NT),
                                       pair_lo[:, 0:NT * NG].rearrange("p (t g) -> p t g", t=NT), ALU.add))
                for t in range(NT):
                    last = dve.max(g_top[:, t, :], gs[:, t, 0:NG])
                done(last)
                done(dve.tensor_copy(g_keep[:, :, 0:TOPG], g_top[:, :, 0:TOPG]))

            def keep_experts():
                for t in range(NT):
                    last = dve.match_replace(g_found[:, t, :], g_keep[:, t, :], gs[:, t, :], BIG)
                done(last)
                done(dve.tensor_scalar(g_mask[:, :, :], g_found[:, :, 0:NG], FOUND, None, ALU.is_ge))
                done(dve.tensor_tensor(sfc[:, :].rearrange("p (g e) -> p g e", e=GE),
                                       sfc[:, :].rearrange("p (g e) -> p g e", e=GE),
                                       g_mask[:, :, :].rearrange("p t g -> p (t g)").unsqueeze(2)
                                       .to_broadcast([P, NT * NG, GE]), ALU.mult))
                for t in range(NT):
                    last = dve.max(e_top[:, t, :], sfc[:, t * E:(t + 1) * E])
                done(last)
                for t in range(NT):
                    last = dve.match_replace(chosen[:, t, :], e_top[:, t, :], sfc[:, t * E:(t + 1) * E], BIG)
                done(last)

            def coefficients(seg, n):
                done(dve.scalar_tensor_tensor(chosen[:, :, :], chosen[:, :, :], FOUND, th[:, :, :],
                                              ALU.is_ge, ALU.mult))
                done(dve.reduce_sum(w_sum[:, :], chosen[:, :, :], AX_X))
                done(dve.tensor_scalar(w_sum[:, :], w_sum[:, :], 1e-20, None, ALU.add))
                done(dve.reciprocal(w_sum[:, :], w_sum[:, :]))
                done(dve.scalar_tensor_tensor(chosen[:, :, :], chosen[:, :, :], 0.5 * ROUTE_SCALE,
                                              w_sum[:, :].unsqueeze(2).to_broadcast([P, NT, E]),
                                              ALU.mult, ALU.mult))
                ch = chosen[:, :, :].rearrange("p t (f e) -> p t f e", f=2)
                part = [coef_parts[:, :, :, a, :] for a in range(PARTS)]
                done(dve.tensor_copy(part[0], ch))
                done(dve.tensor_tensor(ch, ch, part[0], ALU.subtract))
                done(dve.tensor_copy(part[1], ch))
                dve.tensor_tensor(part[2], ch, part[1], ALU.subtract).then_inc(coefparts_done, 1)

            def tasks(seg, base):
                steps[0] = steps[0] if seg is PRO_ else 0
                for kind, n, i in seg.tasks:
                    task = (kind, n, i)
                    par = n % 2
                    if kind == "chunk":
                        _, hi, lo, rows, cols = chunks[i]
                        if lo is None:
                            dve.wait_ge(stage_in[i % 2], 16 * (i // 2 + 1))
                            dve.tensor_copy(hi, hid[0:rows, i % 2, 0:cols]).then_inc(stage_used, 1)
                        else:
                            dve.wait_ge(stage_hi, i + 1)
                            dve.tensor_tensor(lo, hid[0:rows, i % 2, 0:cols], hi.bitcast(F32), ALU.subtract)\
                                .then_inc(stage_used, 1)
                    if kind in ("q", "k"):
                        after(dve, seg, part1_done, ("q", "k"), task)
                        nth = seg.nth(BANK_SM, task)
                        dve.tensor_tensor(rest[:, :], sm[:, :], qk_parts[:, 0, :], ALU.subtract).then_inc(sm_free, 1)
                        dve.wait_ge(sm_free, nth)
                        done(dve.tensor_copy(qk_parts[:, 1, :], rest[:, :]))
                        dve.tensor_tensor(qk_parts[:, 2, :], rest[:, :], qk_parts[:, 1, :], ALU.subtract)\
                            .then_inc(parts_done, 1)
                    if kind == "v":
                        after(dve, seg, sm_full, BANK_SM, task)
                        after(dve, seg, ob_full, BANK_O, ("pv", n - 2, GROUPS - 1))
                        dst = v_sb[:, par, :, 0:NH * VW].rearrange("p t (h e) -> p t h e", e=VW)[:, :, :, 0:C]
                        dve.tensor_copy(dst, sm[:, :].rearrange("p (t h c) -> p t h c", t=NT, c=C))\
                            .then_inc(sm_free, 1)
                    if kind == "mx":
                        h, part = divmod(i, 3)
                        after(dve, seg, sm_full, BANK_SM, task)
                        col = 0
                        for qb in MX_PARTS[part]:
                            wide = (qb + 1) * P
                            last = dve.tensor_tensor_reduce(
                                out=max_out[:, col:col + wide], in0=sm[:, col:col + wide], in1=causal_sb[:, S - wide:S],
                                scale=1.0, scalar=-BIG, op0=ALU.add, op1=ALU.max,
                                accum_out=row_max[:, h % HG, qb:qb + 1])
                            col += wide
                        last.then_inc(sm_free, 1)
                    if kind == "mn":
                        after(dve, seg, sm_free, BANK_SM, ("mx", n, 3 * (HG * i + HG) - 1))
                        rm = row_max[:, :, :].rearrange("p h t -> p (h t)")
                        done(dve.tensor_scalar(max_parts[:, 0, :], rm, -1.0, None, ALU.mult))
                        done(dve.scalar_tensor_tensor(max_rest[:, :], rm, -1.0, max_parts[:, 0, :],
                                                      ALU.mult, ALU.subtract))
                        done(dve.tensor_copy(max_parts[:, 1, :], max_rest[:, :]))
                        dve.tensor_tensor(max_parts[:, 2, :], max_rest[:, :], max_parts[:, 1, :], ALU.subtract)\
                            .then_inc(maxparts_done, 1)
                    if kind == "mT":
                        after(dve, seg, sm_full, BANK_SM, task)
                        before = ("mT", n, i - 1) if i else ("mT", n - 1, GROUPS - 1)
                        if seg.nth(("mT",), before):
                            dve.wait_ge(maxrows_in[before[2]], 16 * PARTS * group_nth(seg, *before))
                        dve.tensor_copy(max_rows[:, :], sm[0:PARTS * HG * NT, 0:P // 2].bitcast(BF16))\
                            .then_inc(sm_free, 1)
                    if kind == "ot":
                        after(dve, seg, ob_full, BANK_O, task)
                        o = ob[:, :].rearrange("p (t j e) -> p t j e", j=HG, e=32)
                        done(dve.reciprocal(rden[:, :, :], o[:, :, :, C]))
                        dst = att[:, :, i * HG * C:(i + 1) * HG * C].rearrange("p t (j c) -> p t j c", c=C)
                        dve.tensor_tensor(dst, o[:, :, :, 0:C], rden[:, :, :].unsqueeze(3)
                                          .to_broadcast([P, NT, HG, C]), ALU.mult).then_inc(ob_free, 1)
                    if kind == "oproj":
                        after(dve, seg, xtok_in, ("ldtok",), ("ldtok", n, 0), 16)
                        norm_stats(seg, task, xtok_sb[:, :, :])
                    if kind == "x1":
                        normalise(seg, ("oproj", n, 0), x1[:, par], x1_done)
                    if kind == "x1T":
                        after(dve, seg, x1hi_done, ("x1T",), task)
                        dve.tensor_tensor(x1_lo[:, par, :], ob[:, :], x1_hi[:, par, :].bitcast(F32),
                                          ALU.subtract).then_inc(ob_free, 1)
                    if kind == "tk":
                        if i == 0:
                            after(dve, seg, ob_free, BANK_O, ("router", n, 0))
                        (group_scores, keep_groups, keep_experts, lambda: coefficients(seg, n))[i]()
                    if kind == "a":
                        after(dve, seg, tanh_done, ("g",), ("g", n, i))
                        dve.scalar_tensor_tensor(hid[:, i % 3, :], hid[:, i % 3, :], 1.0, pg[:, :],
                                                 ALU.add, ALU.mult).then_inc(a_done, 1)
                    if kind == "b":
                        after(dve, seg, a_done, ("a",), ("a", n, i))
                        after(dve, seg, u_full, ("u",), ("u", n, i))
                        if i == SHARED:
                            ins = dve.scalar_tensor_tensor(hid[:, i % 3, :], hid[:, i % 3, :], 0.5, pu[:, :],
                                                           ALU.mult, ALU.mult)
                        else:
                            ins = dve.tensor_tensor(hid[:, i % 3, :], hid[:, i % 3, :], pu[:, :], ALU.mult)
                        ins.then_inc(b_done, 1)
                    if kind == "finT":
                        norm_stats(seg, task, x1[:, par])
                    if kind == "finx":
                        after(dve, seg, out_stored, ("finx",), ("finx", n - 1, 0), 16)
                        normalise(seg, ("finT", n, 0), out_sb, out_ready)

            run(dve, tasks)


def kernel(**inputs):
    import numpy as np
    import concourse.bacc as bacc
    from concourse.bass_utils import run_bass_kernel_spmd

    a = {k.removeprefix("L0_attn_").removeprefix("L0_ffn_"): np.asarray(v) for k, v in inputs.items()}
    e32 = np.arange(STACK)[:, None] % EH == np.arange(EH * I)[None, :] // I
    arrays = {
        "x": a["x"].reshape(B * S, D),
        "xT": a["x"].transpose(0, 2, 1),
        "wqT": a["q_proj_weight"].T, "wkT": a["k_proj_weight"].T, "wvT": a["v_proj_weight"].T,
        "woT": a["o_proj_weight"].T, "rwT": a["router_w"].T, "bias": a["e_bias"],
        "Wg": a["Wg"].transpose(1, 0, 2).reshape(D, E * I),
        "Wu": a["Wu"].transpose(1, 0, 2).reshape(D, E * I),
        "Wd": a["Wd"].reshape(PAIRS, P, D).transpose(1, 0, 2).reshape(P, PAIRS * D),
        "SWg": a["SWg"], "SWu": a["SWu"], "SWd": a["SWd"],
        "ident": np.eye(P, dtype=np.float32),
        "causal": np.where(np.arange(S)[None, :] > np.arange(P)[:, None] + S - P, -BIG, 0.0).astype(np.float32),
        "select": e32.astype(np.float32),
    }
    arrays = {k: np.ascontiguousarray(v) for k, v in arrays.items()}
    nc = bacc.Bacc("TRN2", target_bir_lowering=False, num_devices=1)
    aps = {k: nc.dram_tensor(f"in_{k}", v.shape, mybir.dt.from_np(v.dtype), kind="ExternalInput").ap()
           for k, v in arrays.items()}
    out = nc.dram_tensor("out_0", (B * S, D), F32, kind="ExternalOutput").ap()
    build(nc, out=out, **aps)
    r = run_bass_kernel_spmd(nc, [{f"in_{k}": v for k, v in arrays.items()}], core_ids=[0])
    return r.results[0]["out_0"].reshape(B, S, D)
```

```python
import math
from contextlib import ExitStack

import concourse.bass as bass
from concourse import mybir

F32 = mybir.dt.float32
F32R = mybir.dt.float32r
BF16 = mybir.dt.bfloat16
ALU = mybir.AluOpType
ACT = mybir.ActivationFunctionType
AX_X = mybir.AxisListType.X

P = 128
B, S, D = 8, 512, 128
NH, C = 16, 8
NT = S // P
E, I = 64, 64
PAIRS = E * I // P
SHARED = 0
UNITS = PAIRS + 1
NG = 8
GE = E // NG
TK_STEPS = 20
CONSTS = 4
TOPG, TOPK = 4, 8
ROUTE_SCALE = 2.5
EPS = 1e-5
HG = 4
GROUPS = NH // HG
CHUNKS = 5
PARTS = 3
QK_ROWS = PARTS * PARTS * C
STACK = 96
VW = C + 1
VPAD = NH * VW + 32 - VW
BIG = 3.0e38
FOUND = 1.0e38
HEAD_COLS = 1280
KB_AT = (0, 512, 1024, 896)
ST_PARTS = ((0,), (1, 3), (2,))
MX_PARTS = ((0, 1), (2,), (3,))


def attention_places(max_at, st_at, pace, proj_at, stack_at, tail_at, tk_pace):
    out = [(proj_at - 3.4, "ld", 0), (proj_at, "q", 0), (proj_at + 1, "k", 0), (proj_at + 2, "v", 0),
           (tail_at - 4, "ldtok", 0)]
    for step in range(2):
        out += [(proj_at + 0.5 + 0.4 * step, "qsplit", step),
                (proj_at + 1.5 + 0.4 * step, "ksplit", step)]
    for g in range(GROUPS):
        last = HG * (g + 1) * pace
        out += [(stack_at[g] + 0.02, "rs", g),
                (max_at + last + 0.42 * pace, "mT", g),
                (st_at + last + 0.1 * pace, "pv", g), (st_at + last + 0.42 * pace, "ot", g),
                (st_at + last + 0.54 * pace, "on", g)]
        for step in range(4):
            out.append((max_at + last + (0.12 * step - 0.12) * pace, "mn", 4 * g + step))
    for h in range(NH):
        for part, off in enumerate((0.05, 0.33, 0.55)):
            out.append((max_at + (h + off) * pace, "mx", 3 * h + part))
        for part, off in enumerate((0.2, 0.45, 0.7)):
            out.append((st_at + (h + off) * pace, "st", 3 * h + part))
        out.append((st_at + (h + 0.72) * pace, "mask", h))
    for after_tail, kind, i in ((0.1, "attT", 0), (1.1, "oproj", 0), (1.4, "ln", 0), (1.6, "ln", 1),
                                (1.8, "ln", 2), (2.15, "x1", 0), (2.8, "x1T", 0), (3.7, "router", 0)):
        out.append((tail_at + after_tail, kind, i))
    for step in range(TK_STEPS):
        out.append((tail_at + 4.1 + tk_pace * step, "tk", step))
    out.append((tail_at + 4.3 + tk_pace * TK_STEPS, "coefT", 0))
    return out


STEADY = attention_places(-54, -43, 2, -60, (-57, -56.8, -51.9, -43.9), -10, 0.23)
PACKED = {0: attention_places(5, 12, 1, 0, (2.1, 2.2, 2.3, 2.4), 29, 0.15),
          1: attention_places(23, 31, 1, 14, (19, 23, 24.1, 28.1), 60, 0.15)}
CHUNK_AT = (-3, 3, 5.5, 7.5, 9.5)
BEYOND = 2.5


def moe_places():
    out = []
    for u in range(UNITS):
        out += [(u, "g", u), (u + 0.25, "u", u), (u + 0.3, "a", u), (u + 0.55, "b", u),
                (u + 2.2, "d", u)]
        if u != SHARED:
            out.append((u + 0.6, "h", u))
    for j in range(PAIRS // 2):
        out.append((2 * j - 1.35 if j else -0.7, "c", j))
    out += [(UNITS + 1.25, "fin", 0), (UNITS + 1.7, "finT", 0), (UNITS + 1.8, "ln", 3),
            (UNITS + 2.1, "ln", 4), (UNITS + 2.4, "ln", 5), (UNITS + 2.8, "finx", 0)]
    return out


def order(first_step, last_step, batches):
    out = []
    for n in batches:
        for at, kind, i in STEADY:
            if first_step <= math.floor(n + (at - BEYOND) / UNITS) <= last_step:
                out.append((n * UNITS + at, kind, n, i))
        if first_step <= n <= last_step:
            out += [(n * UNITS + at, kind, n, i) for at, kind, i in moe_places()]
    return [(kind, n, i) for _, kind, n, i in sorted(out, key=lambda x: x[0])]


def prologue_order():
    here = set(order(-2, -1, range(B)))
    out = [(at, kind, n, i) for n in PACKED for at, kind, i in PACKED[n] if (kind, n, i) in here]
    assert len(out) == len(here)
    out += [(at, "chunk", 0, j) for j, at in enumerate(CHUNK_AT)]
    return [(kind, n, i) for _, kind, n, i in sorted(out, key=lambda x: x[0])]


BANK_SM = ("q", "k", "v", "mx", "mT")
BANK_O = ("pv", "ot", "attT", "oproj", "x1T", "router", "coefT", "finT")
LN = ("oproj", "finT")


class Segment:

    def __init__(self, tasks):
        self.tasks = tasks
        self.numbers = {}
        for kinds in (BANK_SM, BANK_O, LN, ("q", "k")) + tuple((k,) for k in {t[0] for t in tasks}):
            here = [t for t in tasks if t[0] in kinds]
            self.numbers[kinds] = {t: n + 1 for n, t in enumerate(here)}

    def nth(self, kinds, task):
        return self.numbers.get(kinds, {}).get(task, 0)

    def total(self, kinds):
        return len(self.numbers.get(kinds, {}))


def build(nc, x, xT, wqT, wkT, wvT, woT, rwT, bias, Wg, Wu, Wd, SWgu, SWd, ident, causal, out):
    x_tok = x.rearrange("(b t p) d -> b p t d", t=NT, p=P)
    out_tok = out.rearrange("(b t p) d -> b p t d", t=NT, p=P)
    q_rows_dram = nc.dram_tensor("q_rows_dram", [NH, PARTS, PARTS, C, S], BF16).ap()
    k_rows_dram = nc.dram_tensor("k_rows_dram", [NH, PARTS, PARTS, C, S], BF16).ap()
    coef_dram = nc.dram_tensor("coef_dram", [2, E, S], F32).ap()

    PRO = Segment(prologue_order())
    BODY = Segment(order(0, 1, range(B)))
    EPI = Segment(order(6, 7, range(B)))
    BODY_RUNS = (B - 2) // 2

    with ExitStack() as ctx:
        def sb(name, shape, dt=F32):
            return ctx.enter_context(nc.sbuf_tensor(name, shape, dt))

        def bank(name):
            return ctx.enter_context(nc.psum_tensor(name, [P, 512], F32))

        sems = []

        def sem(name):
            s = ctx.enter_context(nc.semaphore(name))
            sems.append(s)
            return s

        wg_hi, wg_lo = sb("wg_hi", [P, E * I], F32R), sb("wg_lo", [P, E * I], F32R)
        wu_hi, wu_lo = sb("wu_hi", [P, E * I], F32R), sb("wu_lo", [P, E * I], F32R)
        wd_sb = sb("wd_sb", [P, PAIRS * D])
        sgu_hi, sgu_lo = sb("sgu_hi", [P, 2 * P], F32R), sb("sgu_lo", [P, 2 * P], F32R)
        sd_sb = sb("sd_sb", [P, D])
        wq_sb, wk_sb, wv_sb, wo_sb = (sb(f"w{n}_sb", [P, D]) for n in "qkvo")
        rw_sb = sb("rw_sb", [P, E])
        bias_sb = sb("bias_sb", [P, E])
        id_sb = sb("id_sb", [P, P])
        id_bf = sb("id_bf", [P, P], BF16)
        causal_sb = sb("causal_sb", [P, S], BF16)
        half_power = sb("half_power", [P, NT])
        xT_sb = sb("xT_sb", [P, S])
        xtok_sb = sb("xtok_sb", [P, NT, D])
        qk_parts = sb("qk_parts", [P, 2, PARTS, S], BF16)
        rest = sb("rest", [P, S])
        q_stack = sb("q_stack", [STACK, NH, S], BF16)
        k_stack = sb("k_stack", [STACK, NH, S], BF16)
        v_sb = sb("v_sb", [P, 2, NT, VPAD])
        max_out = sb("max_out", [P, 2, S], BF16)
        row_max = sb("row_max", [P, 2, HG, NT])
        max_rest = sb("max_rest", [P, HG * NT])
        max_parts = sb("max_parts", [P, PARTS, HG * NT], BF16)
        max_rows = sb("max_rows", [PARTS * HG * NT, P], BF16)
        probs = sb("probs", [P, HG, HEAD_COLS])
        ev = sb("ev", [P, S])
        rden = sb("rden", [P, NT, HG])
        att = sb("att", [P, NT, D])
        y = sb("y", [P, NT, D])
        stats = sb("stats", [P, NT, 6])
        mv = sb("mv", [P, NT, 2])
        var_eps = sb("var_eps", [P, NT])
        rstd = sb("rstd", [P, NT])
        x1 = sb("x1", [P, 2, NT, D])
        x1T = sb("x1T", [P, S])
        th = sb("th", [P, NT, E])
        sfc = sb("sfc", [P, NT * E])
        pair_hi = sb("pair_hi", [P, NT * NG * 4])
        pair_lo = sb("pair_lo", [P, NT * NG * 4])
        quad_a = sb("quad_a", [P, NT * NG * 2])
        quad_b = sb("quad_b", [P, NT * NG * 2])
        gs = sb("gs", [P, NT, NG + TOPG])
        g_top = sb("g_top", [P, NT, 8])
        g_keep = sb("g_keep", [P, NT, 8])
        g_found = sb("g_found", [P, NT, NG + TOPG])
        merge_tmp = sb("merge_tmp", [P, NT * NG * 2])
        g_mask = sb("g_mask", [P, NT, NG])
        e_top = sb("e_top", [P, NT, 8])
        chosen = sb("chosen", [P, NT, E])
        w_sum = sb("w_sum", [P, NT])
        coef_T = sb("coef_T", [E, 2, S])
        x1_hi, x1_lo = sb("x1_hi", [P, 2, S], F32R), sb("x1_lo", [P, 2, S], F32R)
        hid = sb("hid", [P, 3, S])
        coef_b = sb("coef_b", [P, 2, 2, S])
        ffn_T = sb("ffn_T", [P, S])
        out_sb = sb("out_sb", [P, NT, D])

        acc, pg, pu, ob = bank("acc"), bank("pg"), bank("pu"), bank("ob")
        sm_bank = bank("sm0"), bank("sm1")
        st_bank = bank("st0"), bank("st1")

        x_in = sem("x_in")
        xtok_in = sem("xtok_in")
        sm_full, sm_free = sem("sm_full"), sem("sm_free")
        ob_full, ob_free = sem("ob_full"), sem("ob_free")
        part1_done = sem("part1_done")
        parts_done = sem("parts_done")
        parts_stored = sem("parts_stored")
        stacked = [sem(f"stacked{g}") for g in range(GROUPS)]
        maxparts_done = sem("maxparts_done")
        maxrows_in = [sem(f"maxrows_in{g}") for g in range(GROUPS)]
        st_full, exp_done = sem("st_full"), sem("exp_done")
        probs_ready = sem("probs_ready")
        var_done, rstd_done, x1_done = sem("var_done"), sem("rstd_done"), sem("x1_done")
        x1hi_done, coef_done = sem("x1hi_done"), sem("coef_done")
        coef_stored = sem("coef_stored")
        c_in = [sem(f"c_in{j}") for j in range(2)]
        g_full, u_full, d_full = sem("g_full"), sem("u_full"), sem("d_full")
        tanh_done, a_done, b_done = sem("tanh_done"), sem("a_done"), sem("b_done")
        h_done = sem("h_done")
        acc_free = sem("acc_free")
        out_ready, out_stored = sem("out_ready"), sem("out_stored")
        dve_step = sem("dve_step")
        wqkv_in = sem("wqkv_in")
        w_in = sem("w_in")
        id_in = sem("id_in")
        stage_in = [sem(f"stage_in{j}") for j in range(3)]
        stage_hi, stage_used = sem("stage_hi"), sem("stage_used")
        zero_done = sem("zero_done")
        const_done = sem("const_done")
        seg_done = ctx.enter_context(nc.semaphore("seg_done"))
        seg_go = ctx.enter_context(nc.semaphore("seg_go"))
        seg_ack = ctx.enter_context(nc.semaphore("seg_ack"))

        wide = E * I // 2
        chunks = [(SWgu, sgu_hi[:, :], sgu_lo[:, :], hid[:, 0, 0:2 * P], 2)]
        flat = probs[:, :, :].rearrange("p h c -> p (h c)")
        for half in range(2):
            cols = slice(half * wide, (half + 1) * wide)
            for slot, (src, hi, lo) in enumerate(((Wg, wg_hi, wg_lo), (Wu, wu_hi, wu_lo))):
                chunks.append((src[:, cols], hi[:, cols], lo[:, cols],
                               flat[:, slot * wide:(slot + 1) * wide], slot))
        assert len(chunks) == CHUNKS

        small = [(wo_sb, woT), (rw_sb, rwT), (bias_sb, bias.unsqueeze(0).to_broadcast([P, E])), (sd_sb, SWd)]

        block = ctx.enter_context(nc.Block())

        def after(eng, seg, s, kinds, task, per=1):
            n = seg.nth(kinds, task)
            if n:
                eng.wait_ge(s, n * per)

        def bank_free(eng, seg, s, kinds, task, banks=1):
            n = seg.nth(kinds, task) - banks
            if n > 0:
                eng.wait_ge(s, n)

        def sm_of(seg, task):
            return sm_bank[seg.nth(BANK_SM, task) % 2]

        def group_nth(seg, kind, n, g):
            return sum(t[0] == kind and t[2] == g and t[1] <= n for t in seg.tasks)

        def end_segment(eng):
            eng.drain().then_inc(seg_done, 1)
            eng.wait_ge(seg_go, 1)
            eng.sem_inc(seg_ack, 1)

        def run(eng, tasks_of, last_too=False):
            tasks_of(PRO, 0)
            end_segment(eng)
            with eng.Fori(0, BODY_RUNS) as i:
                tasks_of(BODY, i * 2)
                end_segment(eng)
            tasks_of(EPI, 0)

        @block.sync
        def _(sp):
            for dst, src in ((wq_sb, wqT), (wk_sb, wkT), (wv_sb, wvT)):
                sp.dma_start(dst[:, :], src).then_inc(wqkv_in, 16)

            def load_chunk(j):
                src, _, _, place, slot = chunks[j]
                if j >= 3:
                    sp.wait_ge(stage_used, j - 1)
                sp.dma_start(place, src).then_inc(stage_in[slot], 16)

            def tasks(seg, base):
                for kind, n, i in seg.tasks:
                    task = (kind, n, i)
                    par = n % 2
                    if kind == "chunk":
                        load_chunk(i)
                        if i == 0:
                            sp.dma_start(id_sb[:, :], ident).then_inc(id_in, 16)
                            sp.dma_start(hid[:, 2, :], causal).then_inc(id_in, 16)
                    if kind == "ld":
                        after(sp, seg, sm_full, BANK_SM, ("v", n - 1, 0))
                        sp.dma_start(xT_sb[:, :], xT[base + n]).then_inc(x_in, 16)
                    if kind == "ldtok":
                        after(sp, seg, ob_free, BANK_O, ("oproj", n - 1, 0))
                        sp.dma_start(xtok_sb[:, :, :], x_tok[base + n]).then_inc(xtok_in, 16)
                    if kind == "v" and seg is PRO and n == 0:
                        for dst, src in small:
                            sp.dma_start(dst[:, :], src).then_inc(w_in, 16)
                    if kind == "mn" and seg is PRO and (n, i) == (0, 0):
                        sp.dma_start(wd_sb[:, :], Wd).then_inc(w_in, 16)
                    if kind in ("qsplit", "ksplit") and i == 1:
                        kind = kind[0]
                        after(sp, seg, parts_done, ("q", "k"), (kind, n, 0))
                        for g in range(GROUPS):
                            if seg.nth(("rs",), ("rs", n - 1, g)):
                                sp.wait_ge(stacked[g], 16 * 2 * group_nth(seg, "rs", n - 1, g))
                        for p in range(PARTS):
                            for other in range(PARTS):
                                dst = q_rows_dram[:, p, other] if kind == "q" else k_rows_dram[:, other, p]
                                sp.dma_start(dst, qk_parts[:, kind == "k", p, :]).then_inc(parts_stored, 16)
                    if kind == "rs" and seg is PRO and (n, i) == (0, 0):
                        sp.wait_ge(zero_done, 3)
                    if kind == "rs":
                        after(sp, seg, parts_stored, ("q", "k"), ("k", n, 0), 16 * PARTS * PARTS)
                        after(sp, seg, st_full, ("st",), ("st", n - 1, 3 * (HG * i + HG) - 1))
                        hs = slice(HG * i, HG * i + HG)
                        for stack, dram in ((q_stack, q_rows_dram), (k_stack, k_rows_dram)):
                            sp.dma_start(stack[0:QK_ROWS, hs, :], dram[hs].rearrange("h a b c t -> (a b c) h t"))\
                                .then_inc(stacked[i], 16)
                    if kind == "mT":
                        after(sp, seg, sm_free, BANK_SM, (kind, n, i))
                        dst = q_stack[QK_ROWS:QK_ROWS + PARTS, HG * i:HG * i + HG, :]
                        sp.dma_start(dst.rearrange("p h (t q) -> p (h t) q", q=P), max_rows[:, :])\
                            .then_inc(maxrows_in[i], 16)
                    if kind == "coefT":
                        after(sp, seg, ob_free, BANK_O, task)
                        sp.dma_start(coef_dram[par], coef_T[:, par, :]).then_inc(coef_stored, 16)
                    if kind == "c":
                        after(sp, seg, coef_stored, ("coefT",), ("coefT", n, 0), 16)
                        before = ("h", n, 2 * i - 2) if i >= 2 else ("h", n - 1, UNITS - 3 + 2 * i)
                        after(sp, seg, h_done, ("h",), before)
                        src = coef_dram[par, 4 * i:4 * i + 4].rearrange("(e j) t -> e (j t)", e=2)
                        sp.dma_start(coef_b[:, i % 2, :, :].rearrange("p j t -> p (j t)"),
                                     src.unsqueeze(0).to_broadcast([I, 2, 2 * S])).then_inc(c_in[i % 2], 16)
                    if kind == "finx":
                        after(sp, seg, out_ready, ("finx",), (kind, n, i))
                        sp.dma_start(out_tok[base + n], out_sb[:, :, :]).then_inc(out_stored, 16)

            def finish(seg, last=False):
                if seg is PRO:
                    sp.wait_ge(w_in, 16 * (len(small) + 1))
                for s, kinds, per in ((x_in, ("ld",), 16), (xtok_in, ("ldtok",), 16),
                                      (parts_stored, ("q", "k"), 16 * PARTS * PARTS),
                                      (coef_stored, ("coefT",), 16), (out_stored, ("finx",), 16)):
                    if seg.total(kinds):
                        sp.wait_ge(s, seg.total(kinds) * per)
                for g in range(GROUPS):
                    for s, kind, per in ((stacked[g], "rs", 16 * 2), (maxrows_in[g], "mT", 16)):
                        many = sum(t[0] == kind and t[2] == g for t in seg.tasks)
                        if many:
                            sp.wait_ge(s, many * per)
                if last:
                    return
                sp.wait_ge(seg_done, 4)
                sp.sem_clear(range(sems[0].num, sems[-1].num + 1))
                sp.sem_clear(seg_done)
                sp.sem_inc(seg_go, 1)
                sp.wait_ge(seg_ack, 4)
                sp.sem_clear(seg_go)
                sp.sem_clear(seg_ack)

            tasks(PRO, 0)
            finish(PRO)
            with sp.Fori(0, BODY_RUNS) as i:
                tasks(BODY, i * 2)
                finish(BODY)
            tasks(EPI, 0)
            finish(EPI, last=True)

        @block.tensor
        def _(pe):
            def split_products(psum, hi, lo, par, first=True):
                pe.matmul(psum[:, :], hi, x1_hi[:, par, :], start=True, stop=False)
                pe.matmul(psum[:, :], hi, x1_lo[:, par, :], start=False, stop=False)
                return pe.matmul(psum[:, :], lo, x1_hi[:, par, :], start=False, stop=True)

            def tasks(seg, base):
                for kind, n, i in seg.tasks:
                    task = (kind, n, i)
                    par = n % 2
                    if kind in BANK_SM:
                        bank_free(pe, seg, sm_free, BANK_SM, task, banks=2)
                        sm = sm_of(seg, task)
                    if kind in BANK_O:
                        bank_free(pe, seg, ob_free, BANK_O, task)
                    if kind == "q" and seg is PRO and n == 0:
                        pe.wait_ge(wqkv_in, 16 * 3)
                    if kind == "mx" and seg is PRO and (n, i) == (0, 0):
                        pe.wait_ge(const_done, CONSTS)
                        pe.wait_ge(zero_done, 3)
                        pe.wait_ge(w_in, 16 * len(small))
                    if kind in ("q", "k"):
                        after(pe, seg, x_in, ("ld",), ("ld", n, 0), 16)
                        w = wq_sb if kind == "q" else wk_sb
                        pe.matmul(sm[:, :], w[:, :], xT_sb[:, :], start=True, stop=True).then_inc(sm_full, 1)
                    if kind == "v":
                        for t in range(NT):
                            mm = pe.matmul(sm[:, t * P:(t + 1) * P], xT_sb[:, t * P:(t + 1) * P], wv_sb[:, :],
                                           start=True, stop=True)
                        mm.then_inc(sm_full, 1)
                    if kind == "mx":
                        h, part = divmod(i, 3)
                        if i % (3 * HG) == 0 and seg.nth(("rs",), ("rs", n, h // HG)):
                            pe.wait_ge(stacked[h // HG], 16 * 2 * group_nth(seg, "rs", n, h // HG))
                        col = 0
                        for qb in MX_PARTS[part]:
                            wide = (qb + 1) * P
                            mm = pe.matmul(sm[:, col:col + wide], q_stack[0:QK_ROWS, h, qb * P:(qb + 1) * P],
                                           k_stack[0:QK_ROWS, h, 0:wide], start=True, stop=True)
                            col += wide
                        mm.then_inc(sm_full, 1)
                    if kind == "mT":
                        after(pe, seg, maxparts_done, ("mT",), task)
                        pe.transpose(sm[0:PARTS * HG * NT, 0:P // 2].bitcast(BF16),
                                     max_parts[:, :, :].rearrange("p a b -> p (a b)"), id_bf[:, :])\
                            .then_inc(sm_full, 1)
                    if kind == "st":
                        h, part = divmod(i, 3)
                        if i % (3 * HG) == 0 and seg.nth(("mT",), ("mT", n, h // HG)):
                            pe.wait_ge(maxrows_in[h // HG], 16 * group_nth(seg, "mT", n, h // HG))
                        bank_free(pe, seg, exp_done, ("st",), task, banks=2)
                        col = 0
                        for kb in ST_PARTS[part]:
                            wide = S - kb * P
                            mm = pe.matmul(st_bank[i % 2][:, col:col + wide], k_stack[:, h, kb * P:(kb + 1) * P],
                                           q_stack[:, h, kb * P:S], start=True, stop=True)
                            col += wide
                        mm.then_inc(st_full, 1)
                    if kind == "pv":
                        after(pe, seg, probs_ready, ("mask",), ("mask", n, HG * i + HG - 1))
                        after(pe, seg, sm_free, BANK_SM, ("v", n, 0))
                        for kb in range(NT):
                            wide = S - kb * P
                            for j in range(HG):
                                c0 = (HG * i + j) * VW
                                mm = pe.matmul(ob[32 * j:32 * j + 32, kb * P:S], v_sb[:, par, kb, c0:c0 + 32],
                                               probs[:, j, KB_AT[kb]:KB_AT[kb] + wide],
                                               start=(kb == 0), stop=(kb == NT - 1))
                        mm.then_inc(ob_full, 1)
                    if kind == "ot" or kind == "attT" or kind == "x1T" or kind == "finT":
                        if kind == "x1T":
                            after(pe, seg, x1_done, ("x1",), ("x1", n, 0))
                        if kind == "finT":
                            after(pe, seg, acc_free, ("fin",), ("fin", n, 0))
                        for t in range(NT):
                            src = {"ot": ev[:, t * P:(t + 1) * P], "attT": att[:, t, :],
                                   "x1T": x1[:, par, t, :], "finT": ffn_T[:, t * P:(t + 1) * P]}[kind]
                            mm = pe.transpose(ob[:, t * P:(t + 1) * P], src, id_sb[:, :])
                        mm.then_inc(ob_full, 1)
                    if kind == "oproj" or kind == "router":
                        lhs, rhs, wide = (ev, wo_sb, D) if kind == "oproj" else (x1T, rw_sb, E)
                        for t in range(NT):
                            mm = pe.matmul(ob[:, t * wide:(t + 1) * wide], lhs[:, t * P:(t + 1) * P], rhs[:, :],
                                           start=True, stop=True)
                        mm.then_inc(ob_full, 1)
                    if kind == "coefT":
                        after(pe, seg, coef_done, ("coefT",), task)
                        for t in range(NT):
                            mm = pe.transpose(ob[0:E, t * P:(t + 1) * P], chosen[:, t, :], id_sb[:, :])
                        mm.then_inc(ob_full, 1)
                    if kind == "g":
                        bank_free(pe, seg, a_done, ("g",), task)
                        after(pe, seg, ob_free, BANK_O, ("x1T", n, 0))
                        w = slice((i - 1) * P, i * P)
                        hi, lo = (sgu_hi[:, 0:P], sgu_lo[:, 0:P]) if i == SHARED else (wg_hi[:, w], wg_lo[:, w])
                        split_products(pg, hi, lo, par).then_inc(g_full, 1)
                    if kind == "u":
                        bank_free(pe, seg, b_done, ("u",), task)
                        w = slice((i - 1) * P, i * P)
                        hi, lo = (sgu_hi[:, P:2 * P], sgu_lo[:, P:2 * P]) if i == SHARED else (wu_hi[:, w], wu_lo[:, w])
                        split_products(pu, hi, lo, par).then_inc(u_full, 1)
                    if kind == "d":
                        if i == SHARED:
                            after(pe, seg, b_done, ("b",), ("b", n, i))
                            after(pe, seg, acc_free, ("fin",), ("fin", n - 1, 0))
                        else:
                            after(pe, seg, h_done, ("h",), ("h", n, i))
                        w = sd_sb[:, :] if i == SHARED else wd_sb[:, (i - 1) * D:i * D]
                        pe.matmul(acc[:, :], w, hid[:, i % 3, :], start=(i == 0), stop=(i == UNITS - 1))\
                            .then_inc(d_full, 1)

            run(pe, tasks)

        @block.scalar
        def _(act):
            def tasks(seg, base):
                for kind, n, i in seg.tasks:
                    task = (kind, n, i)
                    par = n % 2
                    if kind == "chunk":
                        _, hi, _, place, slot = chunks[i]
                        act.wait_ge(stage_in[slot], 32 if i >= 3 else 16)
                        act.activation(hi, place, ACT.Copy).then_inc(stage_hi, 1)
                    if kind in ("q", "k"):
                        after(act, seg, sm_full, BANK_SM, task)
                        after(act, seg, parts_stored, ("q", "k"), ("k", n - 1, 0), 16 * PARTS * PARTS)
                        act.activation(qk_parts[:, kind == "k", 0, :], sm_of(seg, task)[:, :], ACT.Copy).then_inc(part1_done, 1)
                    if kind == "st":
                        h, part = divmod(i, 3)
                        after(act, seg, st_full, ("st",), task)
                        if seg is PRO and (n, i) == (0, 0):
                            act.wait_ge(stage_used, CHUNKS)
                        if part == 0 and h % HG == 0:
                            before = ("pv", n, h // HG - 1) if h else ("pv", n - 1, GROUPS - 1)
                            after(act, seg, ob_full, BANK_O, before)
                        wide = sum(S - kb * P for kb in ST_PARTS[part])
                        at = KB_AT[ST_PARTS[part][0]]
                        act.activation(probs[:, h % HG, at:at + wide], st_bank[i % 2][:, 0:wide], ACT.Exp,
                                       scale=C ** -0.5).then_inc(exp_done, 1)
                    if kind in ("pv", "attT"):
                        after(act, seg, ob_full, BANK_O, task)
                        act.activation(ev[:, :], ob[:, :], ACT.Copy).then_inc(ob_free, 1)
                    if kind == "x1T":
                        after(act, seg, ob_full, BANK_O, task)
                        act.activation(x1T[:, :], ob[:, :], ACT.Copy)
                        after(act, seg, u_full, ("u",), ("u", n - 2, UNITS - 1))
                        act.activation(x1_hi[:, par, :], ob[:, :], ACT.Copy).then_inc(x1hi_done, 1)
                    if kind == "router":
                        after(act, seg, ob_full, BANK_O, task)
                        act.activation(th[:, :, :].rearrange("p t e -> p (t e)"), ob[:, 0:NT * E], ACT.Tanh,
                                       scale=0.5).then_inc(ob_free, 1)
                    if kind == "coefT":
                        after(act, seg, ob_full, BANK_O, task)
                        after(act, seg, coef_stored, ("coefT",), ("coefT", n - 2, 0), 16)
                        act.activation(coef_T[:, par, :], ob[0:E, :], ACT.Copy).then_inc(ob_free, 1)
                    if kind == "g":
                        after(act, seg, g_full, ("g",), task)
                        before = ("d", n, i - 3) if i >= 3 else ("d", n - 1, UNITS + i - 3)
                        after(act, seg, d_full, ("d",), before)
                        act.activation(hid[:, i % 3, :], pg[:, :], ACT.Tanh, scale=0.5).then_inc(tanh_done, 1)
                    if kind == "fin":
                        after(act, seg, d_full, ("d",), ("d", n, UNITS - 1))
                        after(act, seg, ob_full, BANK_O, ("finT", n - 1, 0))
                        act.activation(ffn_T[:, :], acc[:, :], ACT.Copy).then_inc(acc_free, 1)

            run(act, tasks)

        @block.gpsimd
        def _(pool):
            pool.memset(k_stack[64:STACK, :, :], 1.0).then_inc(zero_done, 1)
            pool.wait_ge(zero_done, 1)
            pool.memset(q_stack[64:STACK, :, :], 0.0).then_inc(zero_done, 1)
            pool.wait_ge(zero_done, 2)
            pool.memset(v_sb[:, :, :, :], 0.0).then_inc(zero_done, 1)

            def tasks(seg, base):
                for kind, n, i in seg.tasks:
                    task = (kind, n, i)
                    if kind == "mask":
                        after(pool, seg, exp_done, ("st",), ("st", n, 3 * i + 2))
                        blocks = probs[:, i % HG, :].rearrange("p (a b) -> p a b", b=P)
                        for diagonal in (blocks[:, 0:5:4, :], blocks[:, 7:9, :]):
                            ins = pool.affine_select(out=diagonal, in_=diagonal, compare_op=ALU.is_ge, fill=0.0,
                                                     base=0, pattern=[[0, 2], [1, P]], channel_multiplier=-1)
                        ins.then_inc(probs_ready, 1)
                    if kind == "ln" and i % 3 == 2:
                        after(pool, seg, var_done, LN, ("oproj" if i == 2 else "finT", n, 0))
                        pool.tensor_tensor(rstd[:, :], var_eps[:, :], half_power[:, :], ALU.pow)\
                            .then_inc(rstd_done, 1)
                    if kind == "h":
                        after(pool, seg, b_done, ("b",), ("b", n, i))
                        half, j = divmod(i - 1, 2)
                        many = sum(t[0] == "c" and (t[1], t[2]) <= (n, half) and t[2] % 2 == half % 2
                                   for t in seg.tasks)
                        if many and seg.nth(("c",), ("c", n, half)):
                            pool.wait_ge(c_in[half % 2], 16 * many)
                        pool.tensor_tensor(hid[:, i % 3, :], hid[:, i % 3, :], coef_b[:, half % 2, j, :], ALU.mult)\
                            .then_inc(h_done, 1)

            run(pool, tasks)

        @block.vector
        def _(dve):
            steps = [0]
            last_of = {}

            def done(ins, chain):
                steps[0] += 1
                ins.then_inc(dve_step, 1)
                last_of[chain] = steps[0]

            def ready(chain):
                if chain in last_of:
                    dve.wait_ge(dve_step, last_of[chain])

            dve.memset(half_power[:, :], -0.5).then_inc(const_done, 1)
            dve.memset(gs[:, :, NG:NG + TOPG], -BIG)
            dve.memset(g_keep[:, :, TOPG:8], -BIG)
            dve.wait_ge(id_in, 32)
            dve.tensor_copy(id_bf[:, :], id_sb[:, :]).then_inc(const_done, 1)
            dve.tensor_copy(causal_sb[:, :], hid[:, 2, :]).then_inc(const_done, 1)

            def add_residual(seg, task, x_in):
                after(dve, seg, ob_full, BANK_O, task)
                dve.tensor_tensor(y[:, :, :].rearrange("p t d -> p (t d)"), ob[:, :],
                                  x_in.rearrange("p t d -> p (t d)"), ALU.add).then_inc(ob_free, 1)

            def norm_step(seg, i, task):
                if i == 0:
                    after(dve, seg, ob_free, BANK_O, task)
                    for t in range(NT):
                        last = dve.bn_stats(stats[:, t, :], y[:, t, :])
                    done(last, "ln")
                elif i == 1:
                    ready("ln")
                    for t in range(NT):
                        last = dve.bn_aggr(mv[:, t, :], stats[:, t, :])
                    done(last, "ln")
                else:
                    ready("ln")
                    dve.tensor_scalar(var_eps[:, :], mv[:, :, 1], EPS, None, ALU.add).then_inc(var_done, 1)

            def normalise(seg, task, dst, s):
                after(dve, seg, rstd_done, LN, task)
                for t in range(NT):
                    last = dve.tensor_scalar(dst[:, t, :], y[:, t, :], mv[:, t, 0:1], rstd[:, t:t + 1],
                                             ALU.subtract, ALU.mult)
                last.then_inc(s, 1)

            sfc_groups = sfc[:, :].rearrange("p (g e) -> p g e", e=GE)

            def pairs_of(ap, many):
                both = ap[:, 0:many].rearrange("p (g e) -> p g e", e=2)
                return both[:, :, 0], both[:, :, 1]

            def merge(many, hi, lo, hi_out, lo_out):
                m = many // 2
                dve.tensor_tensor(merge_tmp[:, 0:m], *pairs_of(lo, many), ALU.max)
                dve.tensor_tensor(hi_out[:, 0:m], *pairs_of(hi, many), ALU.max)
                return dve.tensor_tensor(lo_out[:, 0:m], *pairs_of(hi, many), ALU.min)

            def merge_rest(many, lo_out):
                m = many // 2
                return dve.tensor_tensor(lo_out[:, 0:m], lo_out[:, 0:m], merge_tmp[:, 0:m], ALU.max)

            def each_tile(f):
                for t in range(NT):
                    last = f(t)
                return last

            def routing_step(i):
                last = None
                if i == 0:
                    last = dve.tensor_scalar(th[:, :, :], th[:, :, :], 0.5, 0.5, ALU.mult, ALU.add)
                elif i == 1:
                    last = dve.tensor_tensor(sfc[:, :].rearrange("p (t e) -> p t e", t=NT), th[:, :, :],
                                             bias_sb[:, :].unsqueeze(1).to_broadcast([P, NT, E]), ALU.add)
                elif i == 2:
                    dve.tensor_tensor(pair_hi[:, :], *pairs_of(sfc, NT * E), ALU.max)
                    last = dve.tensor_tensor(pair_lo[:, :], *pairs_of(sfc, NT * E), ALU.min)
                elif i == 3:
                    last = merge(NT * E // 2, pair_hi, pair_lo, quad_a, quad_b)
                elif i == 4:
                    last = merge_rest(NT * E // 2, quad_b)
                elif i == 5:
                    last = merge(NT * E // 4, quad_a, quad_b, pair_hi, pair_lo)
                elif i == 6:
                    last = merge_rest(NT * E // 4, pair_lo)
                elif i == 7:
                    last = dve.tensor_tensor(gs[:, :, 0:NG], pair_hi[:, 0:NT * NG].rearrange("p (t g) -> p t g", t=NT),
                                             pair_lo[:, 0:NT * NG].rearrange("p (t g) -> p t g", t=NT), ALU.add)
                elif i == 8:
                    last = each_tile(lambda t: dve.max(g_top[:, t, :], gs[:, t, 0:NG]))
                elif i == 9:
                    last = dve.tensor_copy(g_keep[:, :, 0:TOPG], g_top[:, :, 0:TOPG])
                elif i == 10:
                    last = each_tile(lambda t: dve.match_replace(g_found[:, t, :], g_keep[:, t, :], gs[:, t, :], BIG))
                elif i == 11:
                    last = dve.tensor_scalar(g_mask[:, :, :], g_found[:, :, 0:NG], FOUND, None, ALU.is_ge)
                elif i == 12:
                    last = dve.tensor_tensor(sfc_groups, sfc_groups, g_mask[:, :, :].rearrange("p t g -> p (t g)")
                                             .unsqueeze(2).to_broadcast([P, NT * NG, GE]), ALU.mult)
                elif i == 13:
                    last = each_tile(lambda t: dve.max(e_top[:, t, :], sfc[:, t * E:(t + 1) * E]))
                elif i == 14:
                    last = each_tile(lambda t: dve.match_replace(chosen[:, t, :], e_top[:, t, :],
                                                                 sfc[:, t * E:(t + 1) * E], BIG))
                elif i == 15:
                    last = dve.scalar_tensor_tensor(chosen[:, :, :], chosen[:, :, :], FOUND, th[:, :, :],
                                                    ALU.is_ge, ALU.mult)
                elif i == 16:
                    last = dve.reduce_sum(w_sum[:, :], chosen[:, :, :], AX_X)
                elif i == 17:
                    last = dve.tensor_scalar(w_sum[:, :], w_sum[:, :], 1e-20, None, ALU.add)
                elif i == 18:
                    last = dve.reciprocal(w_sum[:, :], w_sum[:, :])
                else:
                    dve.scalar_tensor_tensor(chosen[:, :, :], chosen[:, :, :], 0.5 * ROUTE_SCALE,
                                             w_sum[:, :].unsqueeze(2).to_broadcast([P, NT, E]),
                                             ALU.mult, ALU.mult).then_inc(coef_done, 1)
                    return
                done(last, "tk")

            def tasks(seg, base):
                steps[0] = 0
                last_of.clear()
                for kind, n, i in seg.tasks:
                    task = (kind, n, i)
                    par = n % 2
                    if kind == "chunk":
                        _, hi, lo, place, _ = chunks[i]
                        dve.wait_ge(stage_hi, i + 1)
                        dve.tensor_tensor(lo, place, hi.bitcast(F32), ALU.subtract).then_inc(stage_used, 1)
                    if kind in ("q", "k"):
                        after(dve, seg, part1_done, ("q", "k"), task)
                        bank_free(dve, seg, parts_done, ("q", "k"), task)
                        dve.tensor_tensor(rest[:, :], sm_of(seg, task)[:, :], qk_parts[:, kind == "k", 0, :],
                                          ALU.subtract).then_inc(sm_free, 1)
                    if kind in ("qsplit", "ksplit"):
                        parts = qk_parts[:, kind == "ksplit"]
                        if i == 0:
                            after(dve, seg, sm_free, BANK_SM, (kind[0], n, 0))
                            done(dve.tensor_copy(parts[:, 1, :], rest[:, :]), kind)
                        else:
                            ready(kind)
                            dve.tensor_tensor(parts[:, 2, :], rest[:, :], parts[:, 1, :], ALU.subtract)\
                                .then_inc(parts_done, 1)
                    if kind == "v" and seg is PRO and n == 0:
                        dve.wait_ge(zero_done, 3)
                        for half in range(2):
                            ones = v_sb[:, half, :, 0:NH * VW].rearrange("p t (h e) -> p t h e", e=VW)[:, :, :, C]
                            last = dve.memset(ones, 1.0)
                        last.then_inc(const_done, 1)
                    if kind == "v":
                        after(dve, seg, sm_full, BANK_SM, task)
                        after(dve, seg, ob_full, BANK_O, ("pv", n - 2, GROUPS - 1))
                        dst = v_sb[:, par, :, 0:NH * VW].rearrange("p t (h e) -> p t h e", e=VW)[:, :, :, 0:C]
                        dve.tensor_copy(dst, sm_of(seg, task)[:, :].rearrange("p (t h c) -> p t h c", t=NT, c=C))\
                            .then_inc(sm_free, 1)
                    if kind == "mx":
                        h, part = divmod(i, 3)
                        after(dve, seg, sm_full, BANK_SM, task)
                        col = 0
                        for qb in MX_PARTS[part]:
                            wide = (qb + 1) * P
                            last = dve.tensor_tensor_reduce(
                                out=max_out[:, seg.nth(BANK_SM, task) % 2, col:col + wide],
                                in0=sm_of(seg, task)[:, col:col + wide], in1=causal_sb[:, S - wide:S],
                                scale=1.0, scalar=-BIG, op0=ALU.add, op1=ALU.max,
                                accum_out=row_max[:, h // HG % 2, h % HG, qb:qb + 1])
                            col += wide
                        last.then_inc(sm_free, 1)
                    if kind == "mn":
                        g, step = divmod(i, 4)
                        rm = row_max[:, g % 2, :, :].rearrange("p h t -> p (h t)")
                        if step == 0:
                            after(dve, seg, sm_free, BANK_SM, ("mx", n, 3 * (HG * g + HG) - 1))
                            done(dve.tensor_scalar(max_parts[:, 0, :], rm, -1.0, None, ALU.mult), "mn")
                        elif step == 1:
                            ready("mn")
                            done(dve.scalar_tensor_tensor(max_rest[:, :], rm, -1.0, max_parts[:, 0, :],
                                                          ALU.mult, ALU.subtract), "mn")
                        elif step == 2:
                            ready("mn")
                            done(dve.tensor_copy(max_parts[:, 1, :], max_rest[:, :]), "mn")
                        else:
                            ready("mn")
                            dve.tensor_tensor(max_parts[:, 2, :], max_rest[:, :], max_parts[:, 1, :],
                                              ALU.subtract).then_inc(maxparts_done, 1)
                    if kind == "mT":
                        after(dve, seg, sm_full, BANK_SM, task)
                        before = ("mT", n, i - 1) if i else ("mT", n - 1, GROUPS - 1)
                        if seg.nth(("mT",), before):
                            dve.wait_ge(maxrows_in[before[2]], 16 * group_nth(seg, *before))
                        dve.tensor_copy(max_rows[:, :], sm_of(seg, task)[0:PARTS * HG * NT, 0:P // 2].bitcast(BF16))\
                            .then_inc(sm_free, 1)
                    if kind == "ot":
                        after(dve, seg, ob_full, BANK_O, task)
                        o = ob[:, :].rearrange("p (t j e) -> p t j e", j=HG, e=32)
                        done(dve.reciprocal(rden[:, :, :], o[:, :, :, C]), "on")
                    if kind == "on":
                        ready("on")
                        o = ob[:, :].rearrange("p (t j e) -> p t j e", j=HG, e=32)
                        dst = att[:, :, i * HG * C:(i + 1) * HG * C].rearrange("p t (j c) -> p t j c", c=C)
                        dve.tensor_tensor(dst, o[:, :, :, 0:C], rden[:, :, :].unsqueeze(3)
                                          .to_broadcast([P, NT, HG, C]), ALU.mult).then_inc(ob_free, 1)
                    if kind == "oproj":
                        after(dve, seg, xtok_in, ("ldtok",), ("ldtok", n, 0), 16)
                        add_residual(seg, task, xtok_sb[:, :, :])
                    if kind == "ln":
                        norm_step(seg, i % 3, ("oproj" if i < 3 else "finT", n, 0))
                    if kind == "x1":
                        normalise(seg, ("oproj", n, 0), x1[:, par], x1_done)
                    if kind == "x1T":
                        after(dve, seg, x1hi_done, ("x1T",), task)
                        dve.tensor_tensor(x1_lo[:, par, :], ob[:, :], x1_hi[:, par, :].bitcast(F32),
                                          ALU.subtract).then_inc(ob_free, 1)
                    if kind == "tk":
                        if i == 0:
                            after(dve, seg, ob_free, BANK_O, ("router", n, 0))
                        else:
                            ready("tk")
                        routing_step(i)
                    if kind == "a":
                        after(dve, seg, tanh_done, ("g",), ("g", n, i))
                        dve.scalar_tensor_tensor(hid[:, i % 3, :], hid[:, i % 3, :], 1.0, pg[:, :],
                                                 ALU.add, ALU.mult).then_inc(a_done, 1)
                    if kind == "b":
                        after(dve, seg, a_done, ("a",), ("a", n, i))
                        after(dve, seg, u_full, ("u",), ("u", n, i))
                        if i == SHARED:
                            ins = dve.scalar_tensor_tensor(hid[:, i % 3, :], hid[:, i % 3, :], 0.5, pu[:, :],
                                                           ALU.mult, ALU.mult)
                        else:
                            ins = dve.tensor_tensor(hid[:, i % 3, :], hid[:, i % 3, :], pu[:, :], ALU.mult)
                        ins.then_inc(b_done, 1)
                    if kind == "finT":
                        add_residual(seg, task, x1[:, par])
                    if kind == "finx":
                        after(dve, seg, out_stored, ("finx",), ("finx", n - 1, 0), 16)
                        normalise(seg, ("finT", n, 0), out_sb, out_ready)

            run(dve, tasks)


def kernel(**inputs):
    import numpy as np
    import concourse.bacc as bacc
    from concourse.bass_utils import run_bass_kernel_spmd

    a = {k.removeprefix("L0_attn_").removeprefix("L0_ffn_"): np.asarray(v) for k, v in inputs.items()}
    quads = {k: a[k].reshape(E // 4, 2, 2, *a[k].shape[1:]) for k in ("Wg", "Wu", "Wd")}
    arrays = {
        "x": a["x"].reshape(B * S, D),
        "xT": a["x"].transpose(0, 2, 1),
        "wqT": a["q_proj_weight"].T, "wkT": a["k_proj_weight"].T, "wvT": a["v_proj_weight"].T,
        "woT": a["o_proj_weight"].T, "rwT": a["router_w"].T, "bias": a["e_bias"],
        "Wg": quads["Wg"].transpose(3, 0, 2, 4, 1).reshape(D, E * I),
        "Wu": quads["Wu"].transpose(3, 0, 2, 4, 1).reshape(D, E * I),
        "Wd": quads["Wd"].transpose(3, 1, 0, 2, 4).reshape(P, PAIRS * D),
        "SWgu": np.concatenate([a["SWg"], a["SWu"]], axis=1), "SWd": a["SWd"],
        "ident": np.eye(P, dtype=np.float32),
        "causal": np.where(np.arange(S)[None, :] > np.arange(P)[:, None] + S - P, -BIG, 0.0).astype(np.float32),
    }
    arrays = {k: np.ascontiguousarray(v) for k, v in arrays.items()}
    nc = bacc.Bacc("TRN2", target_bir_lowering=False, num_devices=1)
    aps = {k: nc.dram_tensor(f"in_{k}", v.shape, mybir.dt.from_np(v.dtype), kind="ExternalInput").ap()
           for k, v in arrays.items()}
    out = nc.dram_tensor("out_0", (B * S, D), F32, kind="ExternalOutput").ap()
    build(nc, out=out, **aps)
    r = run_bass_kernel_spmd(nc, [{f"in_{k}": v for k, v in arrays.items()}], core_ids=[0])
    return r.results[0]["out_0"].reshape(B, S, D)
```

```python
import math
from contextlib import ExitStack

import concourse.bass as bass
from concourse import mybir

F32 = mybir.dt.float32
F32R = mybir.dt.float32r
BF16 = mybir.dt.bfloat16
ALU = mybir.AluOpType
ACT = mybir.ActivationFunctionType
AX_X = mybir.AxisListType.X

P = 128
B, S, D = 8, 512, 128
NH, C = 16, 8
NT = S // P
E, I = 64, 64
PAIRS = E * I // P
SHARED = 0
UNITS = PAIRS + 1
NG = 8
GE = E // NG
TK_STEPS = 20
CONSTS = 5
TOPG = 4
ROUTE_SCALE = 2.5
EPS = 1e-5
HG = 4
GROUPS = NH // HG
RING = 8
STACK_PAIRS = NH // 2
RING_PAIRS = RING // 2
SPLIT_BY_DVE = 3
CHUNKS = 9
PARTS = 3
QK_ROWS = PARTS * PARTS * C
STACK = 96
VW = C + 1
VPAD = NH * VW + 32 - VW
BIG = 3.0e38
FOUND = 1.0e38
HEAD_COLS = 1280
KB_AT = (0, 512, 1024, 896)
ST_PARTS = ((0,), (1, 3), (2,))
MX_PARTS = ((0, 1), (2,), (3,))


HEAD = dict(mx=(0.1, 0.43, 0.75), st=(0.15, 0.25, 0.7), mask=0.82)
PACKED_HEAD = dict(mx=(0.1, 0.28, 0.75), st=(0.2, 0.2, 0.6), mask=0.92)
GROUP = dict(mn=(-0.22, -0.15, 0.02, 0.14), mT=0.42, pv=0.05, ot=0.67, on=0.99)
PACKED_GROUP = dict(mn=(-0.22, -0.2, -0.13, 0.19), mT=0.42, pv=0.1, ot=0.57, on=1.19)
TAIL = dict(attT=0.45, oproj=1.1, ln=(1.25, 1.25, 1.35), x1=2.25, x1T=3.15, router=4.15, tk=4.15, coefT=0.6)
PACKED_TAIL = dict(attT=0.9, oproj=0.9, ln=(1.7, 1.7, 1.8), x1=2.7, x1T=3.7, router=4.15, tk=4.15,
                   coefT=0.8)
MOE_EVEN = dict(u=0.6, a=0.25, b=0.85, d=2.9, h=1.6)
MOE_ODD = dict(u=0.65, a=0.15, b=0.7, d=2.95, h=0.9, hi=1.9, lo=2.0)
FINISH = dict(fin=1.95, finT=2.45, ln=(2.45, 2.5, 2.75), finx=3.75)


def attention_places(max_at, st_at, pace, proj_at, stack_at, tail_at, tk_pace, head, group, tail):
    out = [(proj_at - 3.4, "ld", 0), (proj_at, "q", 0), (proj_at + 1, "k", 0), (proj_at + 2, "v", 0),
           (tail_at - 4, "ldtok", 0)]
    for step in range(2):
        out += [(proj_at + 0.5 + 0.4 * step, "qsplit", step), (proj_at + 1.5 + 0.4 * step, "ksplit", step)]
    for g in range(GROUPS):
        last = HG * (g + 1) * pace
        out += [(max_at + last + group["mT"] * pace, "mT", g)]
        out += [(st_at + last + group[kind] * pace, kind, g) for kind in ("pv", "ot", "on")]
        out += [(max_at + last + off * pace, "mn", 4 * g + step) for step, off in enumerate(group["mn"])]
    for j in range(STACK_PAIRS):
        at = stack_at[j] if j < RING_PAIRS else st_at + 2 * (j - RING_PAIRS + 1) * pace + stack_at[RING_PAIRS]
        out.append((at, "rs", j))
    for h in range(NH):
        out += [(max_at + (h + off) * pace, "mx", 3 * h + part) for part, off in enumerate(head["mx"])]
        out += [(st_at + (h + off) * pace, "st", 3 * h + part) for part, off in enumerate(head["st"])]
        out.append((st_at + (h + head["mask"]) * pace, "mask", h))
    out += [(tail_at + tail[kind], kind, 0) for kind in ("attT", "oproj", "x1", "x1T", "router")]
    out += [(tail_at + at, "ln", step) for step, at in enumerate(tail["ln"])]
    out += [(tail_at + tail["tk"] + tk_pace * step, "tk", step) for step in range(TK_STEPS)]
    coef_at = tail_at + tail["tk"] + tk_pace * TK_STEPS + tail["coefT"]
    out.append((coef_at, "coefT", 0))
    out += [(max(moe_place("h", UNITS + 2 * j - 3) - UNITS, coef_at) + 0.1, "c", j) for j in range(2)]
    return out


def moe_place(kind, u):
    return u + (MOE_ODD if u % 2 else MOE_EVEN)[kind]


STEADY_ARGS = (-55.75, -46.0, 2, -64.5, (-59.15, -52.9, -49.4, -47.4, 0.3), -10.25, 0.27)
PACKED_ARGS = ((5.5, 10.5, 1.05, -3.25, (2.6, 4.3, 8.05, 10.9, 0.55), 27.75, 0.08), (22.25, 27.5, 1.1,
    13.75, (22.25, 24.5, 26.1, 28.35, 0.05), 56.25, 0.22))
STEADY = attention_places(*STEADY_ARGS, HEAD, GROUP, TAIL)
PACKED = {n: attention_places(*args, PACKED_HEAD, PACKED_GROUP, PACKED_TAIL) for n, args in enumerate(PACKED_ARGS)}
BEYOND = 3.25
WEIGHT_LOADS = (-4.9, -4.25, -0.25, 2.9, 5.15, 6.8, 8.95, 12.6, 15.45)
WEIGHT_SPLITS = (-0.09, 2.02, 5.9, 6.7, 9.05, 9.15, 10.1, 15.9, 16.8)


def split_down(u):
    return u % 2 == 1


def moe_places():
    out = []
    for u in range(UNITS):
        if split_down(u):
            out += [(moe_place("hi", u), "hi", u), (moe_place("lo", u), "lo", u)]
        out += [(u, "g", u)] + [(moe_place(kind, u), kind, u) for kind in ("u", "a", "b", "d")]
        if u != SHARED:
            out.append((moe_place("h", u), "h", u))
    for j in range(2, PAIRS // 2):
        out.append((moe_place("h", 2 * j - 2) + 0.05, "c", j))
    out += [(UNITS + FINISH[kind], kind, 0) for kind in ("fin", "finT", "finx")]
    out += [(UNITS + at, "ln", 3 + step) for step, at in enumerate(FINISH["ln"])]
    return out


def order(first_step, last_step, batches):
    out = []
    for n in batches:
        for at, kind, i in STEADY:
            if first_step <= math.floor(n + max((at - BEYOND) / UNITS, -2)) <= last_step:
                out.append((n * UNITS + at, kind, n, i))
        if first_step <= n <= last_step:
            out += [(n * UNITS + at, kind, n, i) for at, kind, i in moe_places()]
    return [(kind, n, i) for _, kind, n, i in sorted(out, key=lambda x: x[0])]


def prologue_order():
    here = set(order(-2, -1, range(B)))
    out = [(at, kind, n, i) for n in PACKED for at, kind, i in PACKED[n] if (kind, n, i) in here]
    assert len(out) == len(here)
    out += [(at, "wld", 0, j) for j, at in enumerate(WEIGHT_LOADS)]
    out += [(at, "chunk", 0, j) for j, at in enumerate(WEIGHT_SPLITS)]
    return [(kind, n, i) for _, kind, n, i in sorted(out, key=lambda x: x[0])]


BANK_SM = ("q", "k", "v", "mx", "mT")
BANK_O = ("pv", "ot", "attT", "oproj", "x1T", "router", "coefT", "finT")
LN = ("oproj", "finT")


class Segment:

    def __init__(self, tasks):
        self.tasks = tasks
        self.numbers = {}
        for kinds in (BANK_SM, BANK_O, LN, ("q", "k")) + tuple((k,) for k in {t[0] for t in tasks}):
            here = [t for t in tasks if t[0] in kinds]
            self.numbers[kinds] = {t: n + 1 for n, t in enumerate(here)}

    def nth(self, kinds, task):
        return self.numbers.get(kinds, {}).get(task, 0)

    def last(self, kinds, task):
        here = [t for t in self.tasks[:self.tasks.index(task)] if t[0] in kinds]
        return here[-1] if here else None

    def total(self, kinds):
        return len(self.numbers.get(kinds, {}))


def build(nc, x, xT, wqT, wkT, wvT, woT, rwT, bias, Wg, Wu, Wd, SWgu, SWd, ident, causal, out):
    x_tok = x.rearrange("(b t p) d -> b p t d", t=NT, p=P)
    out_tok = out.rearrange("(b t p) d -> b p t d", t=NT, p=P)
    q_rows_dram = nc.dram_tensor("q_rows_dram", [2, PARTS, PARTS, C, NH, S], BF16).ap()
    k_rows_dram = nc.dram_tensor("k_rows_dram", [2, PARTS, PARTS, C, NH, S], BF16).ap()
    coef_dram = nc.dram_tensor("coef_dram", [2, E, S], F32).ap()

    PRO = Segment(prologue_order())
    BODY = Segment(order(0, 1, range(B)))
    EPI = Segment(order(6, 7, range(B)))
    BODY_RUNS = (B - 2) // 2

    with ExitStack() as ctx:
        def sb(name, shape, dt=F32):
            return ctx.enter_context(nc.sbuf_tensor(name, shape, dt))

        def bank(name):
            return ctx.enter_context(nc.psum_tensor(name, [P, 512], F32))

        sems = []

        def sem(name):
            s = ctx.enter_context(nc.semaphore(name))
            sems.append(s)
            return s

        wg_hi, wg_lo = sb("wg_hi", [P, E * I], F32R), sb("wg_lo", [P, E * I], F32R)
        wu_hi, wu_lo = sb("wu_hi", [P, E * I], F32R), sb("wu_lo", [P, E * I], F32R)
        wd_hi, wd_lo = sb("wd_hi", [P, PAIRS // 2 * D], F32R), sb("wd_lo", [P, PAIRS // 2 * D], F32R)
        wd_sb = sb("wd_sb", [P, PAIRS // 2 * D])
        sgu_hi, sgu_lo = sb("sgu_hi", [P, 2 * P], F32R), sb("sgu_lo", [P, 2 * P], F32R)
        sd_sb = sb("sd_sb", [P, D])
        wq_sb, wk_sb, wv_sb, wo_sb = (sb(f"w{n}_sb", [P, D]) for n in "qkvo")
        rw_sb = sb("rw_sb", [P, E])
        bias_sb = sb("bias_sb", [P, E])
        id_sb = sb("id_sb", [P, P])
        id_bf = sb("id_bf", [P, P], BF16)
        causal_sb = sb("causal_sb", [P, S], BF16)
        half_power = sb("half_power", [P, NT])
        xT_sb = sb("xT_sb", [P, S])
        qk_parts = sb("qk_parts", [P, 2, PARTS, S], BF16)
        rest = sb("rest", [P, S])
        q_stack = sb("q_stack", [STACK, RING, S], BF16)
        k_stack = sb("k_stack", [STACK, RING, S], BF16)
        v_sb = sb("v_sb", [P, 2, NT, VPAD])
        max_out = sb("max_out", [P, 2, S], BF16)
        row_max = sb("row_max", [P, 2, HG, NT])
        max_rest = sb("max_rest", [P, HG * NT])
        max_parts = sb("max_parts", [P, PARTS, HG * NT], BF16)
        max_rows = sb("max_rows", [PARTS * HG * NT, P], BF16)
        probs = sb("probs", [P, HG, HEAD_COLS])
        ev = sb("ev", [P, S])
        rden = sb("rden", [P, NT, HG])
        att = sb("att", [P, NT, D])
        y = sb("y", [P, NT, D])
        stats = sb("stats", [P, NT, 6])
        mv = sb("mv", [P, NT, 2])
        var_eps = sb("var_eps", [P, NT])
        rstd = sb("rstd", [P, NT])
        x1 = sb("x1", [P, 2, NT, D])
        x1T = sb("x1T", [P, S])
        coef_T = x1T[0:E, :]
        th = sb("th", [P, NT, E])
        sfc = sb("sfc", [P, NT * E])
        pair_hi = sb("pair_hi", [P, NT * NG * 4])
        pair_lo = sb("pair_lo", [P, NT * NG * 4])
        quad_a = sb("quad_a", [P, NT * NG * 2])
        quad_b = sb("quad_b", [P, NT * NG * 2])
        gs = sb("gs", [P, NT, NG + TOPG])
        g_top = sb("g_top", [P, NT, 8])
        g_keep = sb("g_keep", [P, NT, 8])
        g_found = sb("g_found", [P, NT, NG + TOPG])
        merge_tmp = sb("merge_tmp", [P, NT * NG * 2])
        g_mask = sb("g_mask", [P, NT, NG])
        e_top = sb("e_top", [P, NT, 8])
        chosen = sb("chosen", [P, NT, E])
        w_sum = sb("w_sum", [P, NT])
        x1_hi, x1_lo = sb("x1_hi", [P, 2, S], F32R), sb("x1_lo", [P, 2, S], F32R)
        hid = sb("hid", [P, 3, S])
        hid_hi, hid_lo = sb("hid_hi", [P, S], F32R), sb("hid_lo", [P, S], F32R)
        coef_b = sb("coef_b", [P, 2, 2, S])
        out_sb = sb("out_sb", [P, NT, D])

        acc, pg, pu, ob = bank("acc"), bank("pg"), bank("pu"), bank("ob")
        sm_bank = bank("sm0"), bank("sm1")
        st_bank = bank("st0"), bank("st1")

        x_in = sem("x_in")
        xtok_in = sem("xtok_in")
        sm_full, sm_free = sem("sm_full"), sem("sm_free")
        ob_full, ob_free = sem("ob_full"), sem("ob_free")
        part1_done = sem("part1_done")
        parts_done = sem("parts_done")
        parts_stored = sem("parts_stored")
        stacked = [sem(f"stacked{j}") for j in range(RING_PAIRS)]
        maxparts_done = sem("maxparts_done")
        maxrows_in = [sem(f"maxrows_in{g}") for g in range(GROUPS)]
        st_full, exp_done = sem("st_full"), sem("exp_done")
        probs_ready = sem("probs_ready")
        var_done, rstd_done, x1_done = sem("var_done"), sem("rstd_done"), sem("x1_done")
        x1hi_done, coef_done = sem("x1hi_done"), sem("coef_done")
        coef_stored = sem("coef_stored")
        c_in = [sem(f"c_in{j}") for j in range(2)]
        g_full, u_full, d_full = sem("g_full"), sem("u_full"), sem("d_full")
        tanh_done, a_done, b_done = sem("tanh_done"), sem("a_done"), sem("b_done")
        h_done = sem("h_done")
        hidhi_done = sem("hidhi_done")
        low_done = sem("low_done")
        acc_free = sem("acc_free")
        out_ready, out_stored = sem("out_ready"), sem("out_stored")
        dve_step = sem("dve_step")
        wq_in, wkv_in = sem("wq_in"), sem("wkv_in")
        w_in = sem("w_in")
        id_in = sem("id_in")
        split_in = [sem(f"split_in{j}") for j in range(5)]
        hi_done = sem("hi_done")
        lo_done = sem("lo_done")
        waiting_free = sem("waiting_free")
        zero_done = sem("zero_done")
        const_done = sem("const_done")
        seg_done = ctx.enter_context(nc.semaphore("seg_done"))
        seg_go = ctx.enter_context(nc.semaphore("seg_go"))
        seg_ack = ctx.enter_context(nc.semaphore("seg_ack"))
        last_stored = ctx.enter_context(nc.semaphore("last_stored"))

        wide, narrow = E * I // 2, E * I // 4
        waiting = probs[:, :, :].rearrange("p h c -> p (h c)")
        coef_flat = coef_b[:, :, :, :].rearrange("p a j t -> p (a j t)")
        chunks = [(SWgu, sgu_hi[:, :], sgu_lo[:, :], hid[:, 0, 0:2 * P], 0),
                  (Wg[:, 0:wide], wg_hi[:, 0:wide], wg_lo[:, 0:wide], waiting[:, 0:wide], 1),
                  (Wu[:, 0:wide], wu_hi[:, 0:wide], wu_lo[:, 0:wide], waiting[:, wide:2 * wide], 2)]
        for src, hi, lo, parts in ((Wg, wg_hi, wg_lo, (2, 3)), (Wu, wu_hi, wu_lo, (2, 3)), (Wd, wd_hi, wd_lo, (0, 1))):
            for part in parts:
                cols, half = slice(part * narrow, (part + 1) * narrow), part % 2
                chunks.append((src[:, cols], hi[:, cols], lo[:, cols],
                               coef_flat[:, half * narrow:(half + 1) * narrow], 3 + half))
        assert len(chunks) == CHUNKS

        small = [(wo_sb, woT), (rw_sb, rwT), (bias_sb, bias.unsqueeze(0).to_broadcast([P, E])),
                 (sd_sb, SWd), (wd_sb, Wd[:, PAIRS // 2 * D:])]

        block = ctx.enter_context(nc.Block())

        def after(eng, seg, s, kinds, task, per=1):
            n = seg.nth(kinds, task)
            if n:
                eng.wait_ge(s, n * per)

        def bank_free(eng, seg, s, kinds, task, banks=1):
            n = seg.nth(kinds, task) - banks
            if n > 0:
                eng.wait_ge(s, n)

        def sm_of(seg, task):
            return sm_bank[seg.nth(BANK_SM, task) % 2]

        def group_nth(seg, kind, n, g):
            return sum(t[0] == kind and t[2] == g and t[1] <= n for t in seg.tasks)

        def ring_nth(seg, n, j):
            return sum(t[0] == "rs" and t[2] % RING_PAIRS == j % RING_PAIRS and (t[1], t[2]) <= (n, j)
                       for t in seg.tasks)

        def end_segment(eng):
            eng.drain().then_inc(seg_done, 1)
            eng.wait_ge(seg_go, 1)
            eng.sem_inc(seg_ack, 1)

        def run(eng, tasks_of):
            tasks_of(PRO, 0)
            end_segment(eng)
            with eng.Fori(0, BODY_RUNS) as i:
                tasks_of(BODY, i * 2)
                end_segment(eng)
            tasks_of(EPI, 0)

        @block.sync
        def _(sp):
            sp.dma_start(wq_sb[:, :], wqT).then_inc(wq_in, 16)

            def store_part(kind, par, p):
                dst = q_rows_dram[par, p] if kind == "q" else k_rows_dram[par, :, p]
                sp.dma_start(dst.rearrange("o c h t -> (c h) o t"),
                             qk_parts[:, kind == "k", p, :].unsqueeze(1).to_broadcast([P, PARTS, S]))\
                    .then_inc(parts_stored, 16)

            def tasks(seg, base):
                for kind, n, i in seg.tasks:
                    task = (kind, n, i)
                    par = n % 2
                    if kind == "wld":
                        place = chunks[i][4]
                        if i - 2 >= SPLIT_BY_DVE:
                            sp.wait_ge(lo_done, i - 2 - SPLIT_BY_DVE + 1)
                        sp.dma_start(chunks[i][3], chunks[i][0]).then_inc(split_in[place], 16)
                    if kind == "ld":
                        after(sp, seg, sm_full, BANK_SM, ("v", n - 1, 0))
                        sp.dma_start(xT_sb[:, :], xT[base + n]).then_inc(x_in, 16)
                        if seg is PRO and n == 0:
                            sp.dma_start(wk_sb[:, :], wkT).then_inc(wkv_in, 16)
                            sp.dma_start(wv_sb[:, :], wvT).then_inc(wkv_in, 16)
                    if kind == "ldtok":
                        after(sp, seg, x1_done, ("x1",), seg.last(("x1",), task))
                        after(sp, seg, out_ready, ("finx",), seg.last(("finx",), task))
                        sp.dma_start(y[:, :, :], x_tok[base + n]).then_inc(xtok_in, 16)
                    if kind == "q" and seg is PRO and n == 0:
                        sp.dma_start(id_sb[:, :], ident).then_inc(id_in, 16)
                        sp.dma_start(hid[:, 1, :], causal).then_inc(id_in, 16)
                    if kind == "rs" and seg is PRO and (n, i) == (0, 1):
                        for dst, src in small:
                            sp.dma_start(dst[:, :], src).then_inc(w_in, 16)
                    if kind in ("q", "k"):
                        for j in range(STACK_PAIRS - RING_PAIRS, STACK_PAIRS):
                            if seg.nth(("rs",), ("rs", n - 2, j)):
                                sp.wait_ge(stacked[j % RING_PAIRS], 16 * 2 * ring_nth(seg, n - 2, j))
                        after(sp, seg, part1_done, ("q", "k"), task)
                        store_part(kind, par, 0)
                    if kind in ("qsplit", "ksplit") and i == 1:
                        after(sp, seg, parts_done, ("q", "k"), (kind[0], n, 0))
                        for p in range(1, PARTS):
                            store_part(kind[0], par, p)
                    if kind == "rs" and seg is PRO and (n, i) == (0, 0):
                        sp.wait_ge(zero_done, 2)
                        sp.wait_ge(const_done, 1)
                    if kind == "rs":
                        after(sp, seg, parts_stored, ("q", "k"), ("k", n, 0), 16 * PARTS)
                        before = (n, i - RING_PAIRS) if i >= RING_PAIRS else (n - 1, i + STACK_PAIRS - RING_PAIRS)
                        after(sp, seg, st_full, ("st",), ("st", before[0], 3 * 2 * (before[1] + 1) - 1))
                        hs, j = slice(2 * i, 2 * i + 2), i % RING_PAIRS
                        for stack, dram in ((q_stack, q_rows_dram), (k_stack, k_rows_dram)):
                            sp.dma_start(stack[0:QK_ROWS, 2 * j:2 * j + 2, :],
                                         dram[par, :, :, :, hs].rearrange("a b c h t -> (a b c) h t"))\
                                .then_inc(stacked[j], 16)
                    if kind == "mT":
                        after(sp, seg, sm_free, BANK_SM, (kind, n, i))
                        dst = q_stack[QK_ROWS:QK_ROWS + PARTS, HG * i % RING:HG * i % RING + HG, :]
                        sp.dma_start(dst.rearrange("p h (t q) -> p (h t) q", q=P), max_rows[:, :])\
                            .then_inc(maxrows_in[i], 16)
                    if kind == "coefT":
                        after(sp, seg, ob_free, BANK_O, task)
                        sp.dma_start(coef_dram[par], coef_T[:, :]).then_inc(coef_stored, 16)
                    if kind == "c":
                        after(sp, seg, coef_stored, ("coefT",), ("coefT", n, 0), 16)
                        before = ("h", n, 2 * i - 2) if i >= 2 else ("h", n - 1, UNITS - 3 + 2 * i)
                        after(sp, seg, h_done, ("h",), before)
                        src = coef_dram[par, 4 * i:4 * i + 4].rearrange("(e j) t -> e (j t)", e=2)
                        sp.dma_start(coef_b[:, i % 2, :, :].rearrange("p j t -> p (j t)"),
                                     src.unsqueeze(0).to_broadcast([I, 2, 2 * S])).then_inc(c_in[i % 2], 16)
                    if kind == "finx":
                        after(sp, seg, out_ready, ("finx",), (kind, n, i))
                        if seg.nth(("finx",), task) == 1:
                            sp.sem_clear(last_stored)
                        sp.dma_start(out_tok[base + n], out_sb[:, :, :])\
                            .then_inc(last_stored if seg.nth(("finx",), task) == 2 else out_stored, 16)

            def finish(seg, last=False):
                if seg is PRO:
                    sp.wait_ge(w_in, 16 * len(small))
                for s, kinds, per in ((x_in, ("ld",), 16), (xtok_in, ("ldtok",), 16),
                                      (parts_stored, ("q", "k"), 16 * PARTS),
                                      (coef_stored, ("coefT",), 16)):
                    if seg.total(kinds):
                        sp.wait_ge(s, seg.total(kinds) * per)
                for s_all, kind, per in ((stacked, "rs", 16 * 2), (maxrows_in, "mT", 16)):
                    for j, s in enumerate(s_all):
                        many = sum(t[0] == kind and t[2] % len(s_all) == j for t in seg.tasks)
                        if many:
                            sp.wait_ge(s, many * per)
                for half in range(2):
                    many = sum(t[0] == "c" and t[2] % 2 == half for t in seg.tasks)
                    if many:
                        sp.wait_ge(c_in[half], 16 * many)
                if seg.total(("finx",)):
                    sp.wait_ge(out_stored, 16)
                else:
                    sp.sem_inc(last_stored, 16)
                if last:
                    sp.wait_ge(last_stored, 16)
                    return
                sp.wait_ge(seg_done, 4)
                sp.sem_clear(range(sems[0].num, sems[-1].num + 1))
                sp.sem_clear(seg_done)
                sp.sem_inc(seg_go, 1)
                sp.wait_ge(seg_ack, 4)
                sp.sem_clear(seg_go)
                sp.sem_clear(seg_ack)

            tasks(PRO, 0)
            finish(PRO)
            with sp.Fori(0, BODY_RUNS) as i:
                tasks(BODY, i * 2)
                finish(BODY)
            tasks(EPI, 0)
            finish(EPI, last=True)

        @block.tensor
        def _(pe):
            def split_products(psum, hi, lo, par):
                pe.matmul(psum[:, :], hi, x1_hi[:, par, :], start=True, stop=False)
                pe.matmul(psum[:, :], hi, x1_lo[:, par, :], start=False, stop=False)
                return pe.matmul(psum[:, :], lo, x1_hi[:, par, :], start=False, stop=True)

            def tasks(seg, base):
                for kind, n, i in seg.tasks:
                    task = (kind, n, i)
                    par = n % 2
                    if kind in BANK_SM:
                        bank_free(pe, seg, sm_free, BANK_SM, task, banks=2)
                        sm = sm_of(seg, task)
                    if kind in BANK_O:
                        bank_free(pe, seg, ob_free, BANK_O, task)
                    if kind == "q" and seg is PRO and n == 0:
                        pe.wait_ge(wq_in, 16)
                    if kind == "k" and seg is PRO and n == 0:
                        pe.wait_ge(wkv_in, 16 * 2)
                    if kind == "pv" and seg is PRO and (n, i) == (0, 0):
                        pe.wait_ge(w_in, 16 * len(small))
                    if kind == "mx" and seg is PRO and (n, i) == (0, 0):
                        pe.wait_ge(const_done, CONSTS)
                        pe.wait_ge(zero_done, 2)
                    if kind in ("q", "k"):
                        after(pe, seg, x_in, ("ld",), ("ld", n, 0), 16)
                        w = wq_sb if kind == "q" else wk_sb
                        pe.matmul(sm[:, :], w[:, :], xT_sb[:, :], start=True, stop=True).then_inc(sm_full, 1)
                    if kind == "v":
                        for t in range(NT):
                            mm = pe.matmul(sm[:, t * P:(t + 1) * P], xT_sb[:, t * P:(t + 1) * P], wv_sb[:, :],
                                           start=True, stop=True)
                        mm.then_inc(sm_full, 1)
                    if kind == "mx":
                        h, part = divmod(i, 3)
                        if i % (3 * 2) == 0 and seg.nth(("rs",), ("rs", n, h // 2)):
                            pe.wait_ge(stacked[h // 2 % RING_PAIRS], 16 * 2 * ring_nth(seg, n, h // 2))
                        col = 0
                        for qb in MX_PARTS[part]:
                            wide = (qb + 1) * P
                            mm = pe.matmul(sm[:, col:col + wide], q_stack[0:QK_ROWS, h % RING, qb * P:(qb + 1) * P],
                                           k_stack[0:QK_ROWS, h % RING, 0:wide], start=True, stop=True)
                            col += wide
                        mm.then_inc(sm_full, 1)
                    if kind == "mT":
                        after(pe, seg, maxparts_done, ("mT",), task)
                        pe.transpose(sm[0:PARTS * HG * NT, 0:P // 2].bitcast(BF16),
                                     max_parts[:, :, :].rearrange("p a b -> p (a b)"), id_bf[:, :])\
                            .then_inc(sm_full, 1)
                    if kind == "st":
                        h, part = divmod(i, 3)
                        if i % (3 * HG) == 0 and seg.nth(("mT",), ("mT", n, h // HG)):
                            pe.wait_ge(maxrows_in[h // HG], 16 * group_nth(seg, "mT", n, h // HG))
                        bank_free(pe, seg, exp_done, ("st",), task, banks=2)
                        col = 0
                        for kb in ST_PARTS[part]:
                            wide = S - kb * P
                            mm = pe.matmul(st_bank[i % 2][:, col:col + wide], k_stack[:, h % RING, kb * P:(kb + 1) * P],
                                           q_stack[:, h % RING, kb * P:S], start=True, stop=True)
                            col += wide
                        mm.then_inc(st_full, 1)
                    if kind == "pv":
                        after(pe, seg, probs_ready, ("mask",), ("mask", n, HG * i + HG - 1))
                        after(pe, seg, sm_free, BANK_SM, ("v", n, 0))
                        for kb in range(NT):
                            wide = S - kb * P
                            for j in range(HG):
                                c0 = (HG * i + j) * VW
                                mm = pe.matmul(ob[32 * j:32 * j + 32, kb * P:S], v_sb[:, par, kb, c0:c0 + 32],
                                               probs[:, j, KB_AT[kb]:KB_AT[kb] + wide],
                                               start=(kb == 0), stop=(kb == NT - 1))
                        mm.then_inc(ob_full, 1)
                    if kind == "ot" or kind == "attT" or kind == "x1T" or kind == "finT":
                        if kind == "x1T":
                            after(pe, seg, x1_done, ("x1",), ("x1", n, 0))
                        if kind == "finT":
                            after(pe, seg, acc_free, ("fin",), ("fin", n, 0))
                        for t in range(NT):
                            src = {"ot": ev[:, t * P:(t + 1) * P], "attT": att[:, t, :],
                                   "x1T": x1[:, par, t, :], "finT": ev[:, t * P:(t + 1) * P]}[kind]
                            mm = pe.transpose(ob[:, t * P:(t + 1) * P], src, id_sb[:, :])
                        mm.then_inc(ob_full, 1)
                    if kind == "oproj" or kind == "router":
                        lhs, rhs, wide = (ev, wo_sb, D) if kind == "oproj" else (x1T, rw_sb, E)
                        for t in range(NT):
                            mm = pe.matmul(ob[:, t * wide:(t + 1) * wide], lhs[:, t * P:(t + 1) * P], rhs[:, :],
                                           start=True, stop=True)
                        mm.then_inc(ob_full, 1)
                    if kind == "coefT":
                        after(pe, seg, coef_done, ("coefT",), task)
                        for t in range(NT):
                            mm = pe.transpose(ob[0:E, t * P:(t + 1) * P], chosen[:, t, :], id_sb[:, :])
                        mm.then_inc(ob_full, 1)
                    if kind == "g":
                        bank_free(pe, seg, a_done, ("g",), task)
                        after(pe, seg, ob_free, BANK_O, ("x1T", n, 0))
                        w = slice((i - 1) * P, i * P)
                        hi, lo = (sgu_hi[:, 0:P], sgu_lo[:, 0:P]) if i == SHARED else (wg_hi[:, w], wg_lo[:, w])
                        split_products(pg, hi, lo, par).then_inc(g_full, 1)
                    if kind == "u":
                        bank_free(pe, seg, b_done, ("u",), task)
                        w = slice((i - 1) * P, i * P)
                        hi, lo = (sgu_hi[:, P:2 * P], sgu_lo[:, P:2 * P]) if i == SHARED else (wu_hi[:, w], wu_lo[:, w])
                        split_products(pu, hi, lo, par).then_inc(u_full, 1)
                    if kind == "d":
                        if i == SHARED:
                            after(pe, seg, acc_free, ("fin",), ("fin", n - 1, 0))
                        first, last = i == 0, i == UNITS - 1
                        if split_down(i):
                            w = slice(i // 2 * D, (i // 2 + 1) * D)
                            after(pe, seg, low_done, ("lo",), ("lo", n, i))
                            pe.matmul(acc[:, :], wd_hi[:, w], hid_hi[:, :], start=first, stop=False)
                            pe.matmul(acc[:, :], wd_hi[:, w], hid_lo[:, :], start=False, stop=False)
                            pe.matmul(acc[:, :], wd_lo[:, w], hid_hi[:, :], start=False, stop=last)\
                                .then_inc(d_full, 1)
                        else:
                            w = sd_sb[:, :] if i == SHARED else wd_sb[:, (i // 2 - 1) * D:i // 2 * D]
                            if i == SHARED:
                                after(pe, seg, b_done, ("b",), ("b", n, i))
                            else:
                                after(pe, seg, h_done, ("h",), ("h", n, i))
                            pe.matmul(acc[:, :], w, hid[:, i % 3, :], start=first, stop=last).then_inc(d_full, 1)

            run(pe, tasks)

        @block.scalar
        def _(act):
            def tasks(seg, base):
                for kind, n, i in seg.tasks:
                    task = (kind, n, i)
                    par = n % 2
                    if kind == "chunk":
                        _, hi, _, place, at = chunks[i]
                        act.wait_ge(split_in[at], 16 * sum(c[4] == at for c in chunks[:i + 1]))
                        act.activation(hi, place, ACT.Copy).then_inc(hi_done, 1)
                    if kind in ("q", "k"):
                        after(act, seg, sm_full, BANK_SM, task)
                        after(act, seg, parts_stored, ("q", "k"), ("k", n - 1, 0), 16 * PARTS)
                        act.activation(qk_parts[:, kind == "k", 0, :], sm_of(seg, task)[:, :], ACT.Copy)\
                            .then_inc(part1_done, 1)
                    if kind == "st":
                        h, part = divmod(i, 3)
                        after(act, seg, st_full, ("st",), task)
                        if seg is PRO and (n, i) == (0, 0):
                            act.wait_ge(waiting_free, SPLIT_BY_DVE)
                        if part == 0 and h % HG == 0:
                            before = ("pv", n, h // HG - 1) if h else ("pv", n - 1, GROUPS - 1)
                            after(act, seg, ob_full, BANK_O, before)
                        wide = sum(S - kb * P for kb in ST_PARTS[part])
                        at = KB_AT[ST_PARTS[part][0]]
                        act.activation(probs[:, h % HG, at:at + wide], st_bank[i % 2][:, 0:wide], ACT.Exp,
                                       scale=C ** -0.5).then_inc(exp_done, 1)
                    if kind in ("pv", "attT"):
                        after(act, seg, ob_full, BANK_O, task)
                        act.activation(ev[:, :], ob[:, :], ACT.Copy).then_inc(ob_free, 1)
                    if kind == "x1T":
                        after(act, seg, ob_full, BANK_O, task)
                        after(act, seg, coef_stored, ("coefT",), ("coefT", n - 1, 0), 16)
                        act.activation(x1T[:, :], ob[:, :], ACT.Copy)
                        after(act, seg, u_full, ("u",), ("u", n - 2, UNITS - 1))
                        act.activation(x1_hi[:, par, :], ob[:, :], ACT.Copy).then_inc(x1hi_done, 1)
                    if kind == "router":
                        after(act, seg, ob_full, BANK_O, task)
                        act.activation(th[:, :, :].rearrange("p t e -> p (t e)"), ob[:, 0:NT * E], ACT.Tanh,
                                       scale=0.5).then_inc(ob_free, 1)
                    if kind == "coefT":
                        after(act, seg, ob_full, BANK_O, task)
                        act.activation(coef_T[:, :], ob[0:E, :], ACT.Copy).then_inc(ob_free, 1)
                    if kind == "g":
                        after(act, seg, g_full, ("g",), task)
                        before = (n, i - 3) if i >= 3 else (n - 1, UNITS + i - 3)
                        if split_down(before[1]):
                            after(act, seg, low_done, ("lo",), ("lo", *before))
                        else:
                            after(act, seg, d_full, ("d",), ("d", *before))
                        act.activation(hid[:, i % 3, :], pg[:, :], ACT.Tanh, scale=0.5).then_inc(tanh_done, 1)
                    if kind == "hi":
                        after(act, seg, h_done, ("h",), ("h", n, i))
                        before = seg.last(("hi",), task)
                        if before:
                            after(act, seg, d_full, ("d",), ("d", *before[1:]))
                        act.activation(hid_hi[:, :], hid[:, i % 3, :], ACT.Copy).then_inc(hidhi_done, 1)
                    if kind == "fin":
                        after(act, seg, d_full, ("d",), ("d", n, UNITS - 1))
                        after(act, seg, ob_full, BANK_O, seg.last(("ot", "oproj", "finT"), task))
                        act.activation(ev[:, :], acc[:, :], ACT.Copy).then_inc(acc_free, 1)

            run(act, tasks)

        @block.gpsimd
        def _(pool):
            pool.memset(k_stack[64:STACK, :, :], 1.0).then_inc(zero_done, 1)
            pool.wait_ge(zero_done, 1)
            pool.memset(v_sb[:, :, :, :], 0.0).then_inc(zero_done, 1)

            def tasks(seg, base):
                for kind, n, i in seg.tasks:
                    task = (kind, n, i)
                    if kind == "chunk" and i >= SPLIT_BY_DVE:
                        _, hi, lo, place, _ = chunks[i]
                        pool.wait_ge(hi_done, i + 1)
                        pool.tensor_tensor(lo, place, hi.bitcast(F32), ALU.subtract).then_inc(lo_done, 1)
                    if kind == "mask":
                        after(pool, seg, exp_done, ("st",), ("st", n, 3 * i + 2))
                        blocks = probs[:, i % HG, :].rearrange("p (a b) -> p a b", b=P)
                        for diagonal in (blocks[:, 0:5:4, :], blocks[:, 7:9, :]):
                            ins = pool.affine_select(out=diagonal, in_=diagonal, compare_op=ALU.is_ge, fill=0.0,
                                                     base=0, pattern=[[0, 2], [1, P]], channel_multiplier=-1)
                        ins.then_inc(probs_ready, 1)
                    if kind == "ln" and i % 3 == 2:
                        after(pool, seg, var_done, LN, ("oproj" if i == 2 else "finT", n, 0))
                        pool.tensor_tensor(rstd[:, :], var_eps[:, :], half_power[:, :], ALU.pow)\
                            .then_inc(rstd_done, 1)
                    if kind == "h":
                        after(pool, seg, b_done, ("b",), ("b", n, i))
                        half, j = divmod(i - 1, 2)
                        many = sum(t[0] == "c" and (t[1], t[2]) <= (n, half) and t[2] % 2 == half % 2
                                   for t in seg.tasks)
                        if many and seg.nth(("c",), ("c", n, half)):
                            pool.wait_ge(c_in[half % 2], 16 * many)
                        pool.tensor_tensor(hid[:, i % 3, :], hid[:, i % 3, :], coef_b[:, half % 2, j, :], ALU.mult)\
                            .then_inc(h_done, 1)
                    if kind == "lo":
                        after(pool, seg, hidhi_done, ("hi",), ("hi", n, i))
                        pool.tensor_tensor(hid_lo[:, :], hid[:, i % 3, :], hid_hi[:, :].bitcast(F32),
                                           ALU.subtract).then_inc(low_done, 1)

            run(pool, tasks)

        @block.vector
        def _(dve):
            steps = [0]
            last_of = {}

            def done(ins, chain):
                steps[0] += 1
                ins.then_inc(dve_step, 1)
                last_of[chain] = steps[0]

            def ready(chain):
                if chain in last_of:
                    dve.wait_ge(dve_step, last_of[chain])

            dve.memset(q_stack[64:STACK, :, :], 0.0).then_inc(const_done, 1)
            dve.memset(half_power[:, :], -0.5).then_inc(const_done, 1)
            dve.memset(gs[:, :, NG:NG + TOPG], -BIG)
            dve.memset(g_keep[:, :, TOPG:8], -BIG)

            def add_residual(seg, task, x_in):
                after(dve, seg, ob_full, BANK_O, task)
                dve.tensor_tensor(y[:, :, :].rearrange("p t d -> p (t d)"), ob[:, :],
                                  x_in.rearrange("p t d -> p (t d)"), ALU.add).then_inc(ob_free, 1)

            def norm_step(seg, i, task):
                if i == 0:
                    after(dve, seg, ob_free, BANK_O, task)
                    for t in range(NT):
                        last = dve.bn_stats(stats[:, t, :], y[:, t, :])
                    done(last, "ln")
                elif i == 1:
                    ready("ln")
                    for t in range(NT):
                        last = dve.bn_aggr(mv[:, t, :], stats[:, t, :])
                    done(last, "ln")
                else:
                    ready("ln")
                    dve.tensor_scalar(var_eps[:, :], mv[:, :, 1], EPS, None, ALU.add).then_inc(var_done, 1)

            def normalise(seg, task, dst, s):
                after(dve, seg, rstd_done, LN, task)
                for t in range(NT):
                    last = dve.tensor_scalar(dst[:, t, :], y[:, t, :], mv[:, t, 0:1], rstd[:, t:t + 1],
                                             ALU.subtract, ALU.mult)
                last.then_inc(s, 1)

            sfc_groups = sfc[:, :].rearrange("p (g e) -> p g e", e=GE)

            def pairs_of(ap, many):
                both = ap[:, 0:many].rearrange("p (g e) -> p g e", e=2)
                return both[:, :, 0], both[:, :, 1]

            def merge(many, hi, lo, hi_out, lo_out):
                m = many // 2
                dve.tensor_tensor(merge_tmp[:, 0:m], *pairs_of(lo, many), ALU.max)
                dve.tensor_tensor(hi_out[:, 0:m], *pairs_of(hi, many), ALU.max)
                return dve.tensor_tensor(lo_out[:, 0:m], *pairs_of(hi, many), ALU.min)

            def merge_rest(many, lo_out):
                m = many // 2
                return dve.tensor_tensor(lo_out[:, 0:m], lo_out[:, 0:m], merge_tmp[:, 0:m], ALU.max)

            def each_tile(f):
                for t in range(NT):
                    last = f(t)
                return last

            def routing_step(i):
                last = None
                if i == 0:
                    last = dve.tensor_scalar(th[:, :, :], th[:, :, :], 0.5, 0.5, ALU.mult, ALU.add)
                elif i == 1:
                    last = dve.tensor_tensor(sfc[:, :].rearrange("p (t e) -> p t e", t=NT), th[:, :, :],
                                             bias_sb[:, :].unsqueeze(1).to_broadcast([P, NT, E]), ALU.add)
                elif i == 2:
                    dve.tensor_tensor(pair_hi[:, :], *pairs_of(sfc, NT * E), ALU.max)
                    last = dve.tensor_tensor(pair_lo[:, :], *pairs_of(sfc, NT * E), ALU.min)
                elif i == 3:
                    last = merge(NT * E // 2, pair_hi, pair_lo, quad_a, quad_b)
                elif i == 4:
                    last = merge_rest(NT * E // 2, quad_b)
                elif i == 5:
                    last = merge(NT * E // 4, quad_a, quad_b, pair_hi, pair_lo)
                elif i == 6:
                    last = merge_rest(NT * E // 4, pair_lo)
                elif i == 7:
                    last = dve.tensor_tensor(gs[:, :, 0:NG], pair_hi[:, 0:NT * NG].rearrange("p (t g) -> p t g", t=NT),
                                             pair_lo[:, 0:NT * NG].rearrange("p (t g) -> p t g", t=NT), ALU.add)
                elif i == 8:
                    last = each_tile(lambda t: dve.max(g_top[:, t, :], gs[:, t, 0:NG]))
                elif i == 9:
                    last = dve.tensor_copy(g_keep[:, :, 0:TOPG], g_top[:, :, 0:TOPG])
                elif i == 10:
                    last = each_tile(lambda t: dve.match_replace(g_found[:, t, :], g_keep[:, t, :], gs[:, t, :], BIG))
                elif i == 11:
                    last = dve.tensor_scalar(g_mask[:, :, :], g_found[:, :, 0:NG], FOUND, None, ALU.is_ge)
                elif i == 12:
                    last = dve.tensor_tensor(sfc_groups, sfc_groups, g_mask[:, :, :].rearrange("p t g -> p (t g)")
                                             .unsqueeze(2).to_broadcast([P, NT * NG, GE]), ALU.mult)
                elif i == 13:
                    last = each_tile(lambda t: dve.max(e_top[:, t, :], sfc[:, t * E:(t + 1) * E]))
                elif i == 14:
                    last = each_tile(lambda t: dve.match_replace(chosen[:, t, :], e_top[:, t, :],
                                                                 sfc[:, t * E:(t + 1) * E], BIG))
                elif i == 15:
                    last = dve.scalar_tensor_tensor(chosen[:, :, :], chosen[:, :, :], FOUND, th[:, :, :],
                                                    ALU.is_ge, ALU.mult)
                elif i == 16:
                    last = dve.reduce_sum(w_sum[:, :], chosen[:, :, :], AX_X)
                elif i == 17:
                    last = dve.tensor_scalar(w_sum[:, :], w_sum[:, :], 1e-20, None, ALU.add)
                elif i == 18:
                    last = dve.reciprocal(w_sum[:, :], w_sum[:, :])
                else:
                    dve.scalar_tensor_tensor(chosen[:, :, :], chosen[:, :, :], 0.5 * ROUTE_SCALE,
                                             w_sum[:, :].unsqueeze(2).to_broadcast([P, NT, E]),
                                             ALU.mult, ALU.mult).then_inc(coef_done, 1)
                    return
                done(last, "tk")

            def tasks(seg, base):
                steps[0] = 0
                last_of.clear()
                for kind, n, i in seg.tasks:
                    task = (kind, n, i)
                    par = n % 2
                    if kind == "chunk" and i < SPLIT_BY_DVE:
                        _, hi, lo, place, _ = chunks[i]
                        dve.wait_ge(hi_done, i + 1)
                        dve.tensor_tensor(lo, place, hi.bitcast(F32), ALU.subtract).then_inc(waiting_free, 1)
                    if kind in ("q", "k"):
                        after(dve, seg, part1_done, ("q", "k"), task)
                        bank_free(dve, seg, parts_done, ("q", "k"), task)
                        dve.tensor_tensor(rest[:, :], sm_of(seg, task)[:, :], qk_parts[:, kind == "k", 0, :],
                                          ALU.subtract).then_inc(sm_free, 1)
                    if kind in ("qsplit", "ksplit"):
                        parts = qk_parts[:, kind == "ksplit"]
                        if i == 0:
                            after(dve, seg, sm_free, BANK_SM, (kind[0], n, 0))
                            done(dve.tensor_copy(parts[:, 1, :], rest[:, :]), kind)
                        else:
                            ready(kind)
                            dve.tensor_tensor(parts[:, 2, :], rest[:, :], parts[:, 1, :], ALU.subtract)\
                                .then_inc(parts_done, 1)
                    if kind == "v" and seg is PRO and n == 0:
                        dve.wait_ge(id_in, 32)
                        dve.tensor_copy(id_bf[:, :], id_sb[:, :]).then_inc(const_done, 1)
                        dve.tensor_copy(causal_sb[:, :], hid[:, 1, :]).then_inc(const_done, 1)
                        dve.wait_ge(zero_done, 2)
                        for half in range(2):
                            ones = v_sb[:, half, :, 0:NH * VW].rearrange("p t (h e) -> p t h e", e=VW)[:, :, :, C]
                            last = dve.memset(ones, 1.0)
                        last.then_inc(const_done, 1)
                    if kind == "v":
                        after(dve, seg, sm_full, BANK_SM, task)
                        after(dve, seg, ob_full, BANK_O, ("pv", n - 2, GROUPS - 1))
                        dst = v_sb[:, par, :, 0:NH * VW].rearrange("p t (h e) -> p t h e", e=VW)[:, :, :, 0:C]
                        dve.tensor_copy(dst, sm_of(seg, task)[:, :].rearrange("p (t h c) -> p t h c", t=NT, c=C))\
                            .then_inc(sm_free, 1)
                    if kind == "mx":
                        h, part = divmod(i, 3)
                        after(dve, seg, sm_full, BANK_SM, task)
                        col = 0
                        for qb in MX_PARTS[part]:
                            wide = (qb + 1) * P
                            last = dve.tensor_tensor_reduce(
                                out=max_out[:, seg.nth(BANK_SM, task) % 2, col:col + wide],
                                in0=sm_of(seg, task)[:, col:col + wide], in1=causal_sb[:, S - wide:S],
                                scale=1.0, scalar=-BIG, op0=ALU.add, op1=ALU.max,
                                accum_out=row_max[:, h // HG % 2, h % HG, qb:qb + 1])
                            col += wide
                        last.then_inc(sm_free, 1)
                    if kind == "mn":
                        g, step = divmod(i, 4)
                        rm = row_max[:, g % 2, :, :].rearrange("p h t -> p (h t)")
                        if step == 0:
                            after(dve, seg, sm_free, BANK_SM, ("mx", n, 3 * (HG * g + HG) - 1))
                            done(dve.tensor_scalar(max_parts[:, 0, :], rm, -1.0, None, ALU.mult), "mn")
                        elif step == 1:
                            ready("mn")
                            done(dve.scalar_tensor_tensor(max_rest[:, :], rm, -1.0, max_parts[:, 0, :],
                                                          ALU.mult, ALU.subtract), "mn")
                        elif step == 2:
                            ready("mn")
                            done(dve.tensor_copy(max_parts[:, 1, :], max_rest[:, :]), "mn")
                        else:
                            ready("mn")
                            dve.tensor_tensor(max_parts[:, 2, :], max_rest[:, :], max_parts[:, 1, :],
                                              ALU.subtract).then_inc(maxparts_done, 1)
                    if kind == "mT":
                        after(dve, seg, sm_full, BANK_SM, task)
                        before = ("mT", n, i - 1) if i else ("mT", n - 1, GROUPS - 1)
                        if seg.nth(("mT",), before):
                            dve.wait_ge(maxrows_in[before[2]], 16 * group_nth(seg, *before))
                        dve.tensor_copy(max_rows[:, :], sm_of(seg, task)[0:PARTS * HG * NT, 0:P // 2].bitcast(BF16))\
                            .then_inc(sm_free, 1)
                    if kind == "ot":
                        after(dve, seg, ob_full, BANK_O, task)
                        o = ob[:, :].rearrange("p (t j e) -> p t j e", j=HG, e=32)
                        done(dve.reciprocal(rden[:, :, :], o[:, :, :, C]), "on")
                    if kind == "on":
                        ready("on")
                        o = ob[:, :].rearrange("p (t j e) -> p t j e", j=HG, e=32)
                        dst = att[:, :, i * HG * C:(i + 1) * HG * C].rearrange("p t (j c) -> p t j c", c=C)
                        dve.tensor_tensor(dst, o[:, :, :, 0:C], rden[:, :, :].unsqueeze(3)
                                          .to_broadcast([P, NT, HG, C]), ALU.mult).then_inc(ob_free, 1)
                    if kind == "oproj":
                        after(dve, seg, xtok_in, ("ldtok",), ("ldtok", n, 0), 16)
                        add_residual(seg, task, y[:, :, :])
                    if kind == "ln":
                        norm_step(seg, i % 3, ("oproj" if i < 3 else "finT", n, 0))
                    if kind == "x1":
                        normalise(seg, ("oproj", n, 0), x1[:, par], x1_done)
                    if kind == "x1T":
                        after(dve, seg, x1hi_done, ("x1T",), task)
                        dve.tensor_tensor(x1_lo[:, par, :], ob[:, :], x1_hi[:, par, :].bitcast(F32),
                                          ALU.subtract).then_inc(ob_free, 1)
                    if kind == "tk":
                        if i == 0:
                            after(dve, seg, ob_free, BANK_O, ("router", n, 0))
                        else:
                            ready("tk")
                        routing_step(i)
                    if kind == "a":
                        after(dve, seg, tanh_done, ("g",), ("g", n, i))
                        dve.scalar_tensor_tensor(hid[:, i % 3, :], hid[:, i % 3, :], 1.0, pg[:, :],
                                                 ALU.add, ALU.mult).then_inc(a_done, 1)
                    if kind == "b":
                        after(dve, seg, a_done, ("a",), ("a", n, i))
                        after(dve, seg, u_full, ("u",), ("u", n, i))
                        if i == SHARED:
                            ins = dve.scalar_tensor_tensor(hid[:, i % 3, :], hid[:, i % 3, :], 0.5, pu[:, :],
                                                           ALU.mult, ALU.mult)
                        else:
                            ins = dve.tensor_tensor(hid[:, i % 3, :], hid[:, i % 3, :], pu[:, :], ALU.mult)
                        ins.then_inc(b_done, 1)
                    if kind == "finT":
                        add_residual(seg, task, x1[:, par])
                    if kind == "finx":
                        dve.wait_ge(last_stored if seg.nth(("finx",), task) == 1 else out_stored, 16)
                        normalise(seg, ("finT", n, 0), out_sb, out_ready)

            run(dve, tasks)


def kernel(**inputs):
    import numpy as np
    import concourse.bacc as bacc
    from concourse.bass_utils import run_bass_kernel_spmd

    a = {k.removeprefix("L0_attn_").removeprefix("L0_ffn_"): np.asarray(v) for k, v in inputs.items()}
    quads = {k: a[k].reshape(E // 4, 2, 2, *a[k].shape[1:]) for k in ("Wg", "Wu", "Wd")}
    arrays = {
        "x": a["x"].reshape(B * S, D),
        "xT": a["x"].transpose(0, 2, 1),
        **{f"w{n}T": a[f"{n}_proj_weight"].reshape(NH, C, D).transpose(1, 0, 2).reshape(D, D).T for n in "qk"},
         "wvT": a["v_proj_weight"].T,
        "woT": a["o_proj_weight"].T, "rwT": a["router_w"].T, "bias": a["e_bias"],
        "Wg": quads["Wg"].transpose(3, 0, 2, 4, 1).reshape(D, E * I),
        "Wu": quads["Wu"].transpose(3, 0, 2, 4, 1).reshape(D, E * I),
        "Wd": quads["Wd"].transpose(3, 1, 2, 0, 4).reshape(P, PAIRS * D),
        "SWgu": np.concatenate([a["SWg"], a["SWu"]], axis=1), "SWd": a["SWd"],
        "ident": np.eye(P, dtype=np.float32),
        "causal": np.where(np.arange(S)[None, :] > np.arange(P)[:, None] + S - P, -BIG, 0.0).astype(np.float32),
    }
    arrays = {k: np.ascontiguousarray(v) for k, v in arrays.items()}
    nc = bacc.Bacc("TRN2", target_bir_lowering=False, num_devices=1)
    aps = {k: nc.dram_tensor(f"in_{k}", v.shape, mybir.dt.from_np(v.dtype), kind="ExternalInput").ap()
           for k, v in arrays.items()}
    out = nc.dram_tensor("out_0", (B * S, D), F32, kind="ExternalOutput").ap()
    build(nc, out=out, **aps)
    r = run_bass_kernel_spmd(nc, [{f"in_{k}": v for k, v in arrays.items()}], core_ids=[0])
    return r.results[0]["out_0"].reshape(B, S, D)
```
